# Optimizing a Trainium2 kernel written in Bass

```python
import numpy as np
import jax
import jax.numpy as jnp

def _softmax(x, axis=-1):
    return jax.nn.softmax(x, axis=axis)

def _gelu(x):
    return jax.nn.gelu(x, approximate=True)

def _silu(x):
    return jax.nn.silu(x)

def _sigmoid(x):
    return jax.nn.sigmoid(x)

def _layernorm(x, axis=-1, eps=1e-05):
    m = jnp.mean(x, axis=axis, keepdims=True)
    v = jnp.var(x, axis=axis, keepdims=True)
    return (x - m) / jnp.sqrt(v + eps)

def _scatter_add(tgt, idx, src, axis=0):
    return tgt.at[idx].add(src)

def _segment_sum(src, seg, n):
    return jax.ops.segment_sum(src, seg, n)
kernel_name = 'mk_xattn_ffn_d1_seqx_r4_cc21e9'

def setup_inputs(seed: int=0):
    np.random.seed(seed)
    _w = jnp.asarray

    def _rec_inputs():
        import jax
        import jax.numpy as jnp
        _rk = jax.random.key(seed)
        x = 7.22e-05 + 1 * jax.random.normal(jax.random.fold_in(_rk, 1), (32, 128, 1024), jnp.float32)
        _lenS = 128 - jax.random.randint(jax.random.fold_in(_rk, 7), (32,), 0, max(1, 128 // 4) + 1, jnp.int32)
        _lenS2 = 128 - jax.random.randint(jax.random.fold_in(_rk, 8), (32,), 0, max(1, 128 // 4) + 1, jnp.int32)
        _ctx_4096P = jax.random.normal(jax.random.fold_in(_rk, 11), (32, 16, 1024), jnp.float32)
        _ctx_4096c = jax.random.dirichlet(jax.random.fold_in(_rk, 511), 0.3 * jnp.ones((16,), jnp.float32), (32, 128))
        _ctx_4096t = jnp.einsum('bsk,bkd->bsd', _ctx_4096c, _ctx_4096P)
        _ctx_4096t = _ctx_4096t * jax.lax.rsqrt(jnp.mean(jnp.square(_ctx_4096t)) + 1e-12) * 0.953939
        ctx_4096 = 4.13588e-05 + 0.999923 * (_ctx_4096t + 0.3 * jax.random.normal(jax.random.fold_in(_rk, 611), (32, 128, 1024), jnp.float32))
        return (x, ctx_4096)
    x, ctx_4096 = _rec_inputs()

    def _L0_xattn_setup():
        import jax, jax.numpy as jnp
        import numpy as np
        HEADS = 8
        WINDOW = 16

        def _pointwise(W, b, t):
            return jnp.einsum('oc,bct->bot', W, t) + b[None, :, None]
        key = jax.random.key(seed)
        ks = jax.random.split(key, 10)
        B, C, T = (4, 128, 1024)
        s = 0.02
        return {'x': jax.random.normal(ks[0], (B, C, T), jnp.float32), 'cond': jax.random.normal(ks[1], (B, C, T), jnp.float32), 'Wq': jax.random.normal(ks[2], (C, C), jnp.float32) * s, 'bq': jnp.zeros((C,), jnp.float32), 'Wk': jax.random.normal(ks[3], (C, C), jnp.float32) * s, 'bk': jnp.zeros((C,), jnp.float32), 'Wv': jax.random.normal(ks[4], (C, C), jnp.float32) * s, 'bv': jnp.zeros((C,), jnp.float32), 'Wo': jax.random.normal(ks[5], (C, C), jnp.float32) * s, 'bo': jnp.zeros((C,), jnp.float32)}
    _L0_xattn_all = _L0_xattn_setup()
    _L0_xattn_in = {k: v for k, v in _L0_xattn_all.items() if k in ('Wq', 'bq', 'Wk', 'bk', 'Wv', 'bv', 'Wo', 'bo')}
    del _L0_xattn_all

    def _L0_ffn_setup():
        import jax, jax.numpy as jnp
        import numpy as np
        N_EXPERTS = 8
        TOP_K = 2
        D_MODEL = 1024
        RANK = 64
        key = jax.random.key(seed)
        k0, k1, k2, k3 = jax.random.split(key, 4)
        inputs = jax.random.normal(k0, (4, 512, D_MODEL), dtype=jnp.float32)
        gate_w = jax.random.normal(k1, (N_EXPERTS, D_MODEL), dtype=jnp.float32) * 0.02
        lora_A = jax.random.normal(k2, (N_EXPERTS, RANK, D_MODEL), dtype=jnp.float32) * 0.02
        lora_B = jax.random.normal(k3, (N_EXPERTS, D_MODEL, RANK), dtype=jnp.float32) * 0.02
        return {'inputs': inputs, 'gate_w': gate_w, 'lora_A': lora_A, 'lora_B': lora_B}
    _L0_ffn_all = _L0_ffn_setup()
    _L0_ffn_in = {k: v for k, v in _L0_ffn_all.items() if k in ('gate_w', 'lora_A', 'lora_B')}
    del _L0_ffn_all
    return {'x': x, 'ctx_4096': ctx_4096, 'L0_xattn_Wq': _L0_xattn_in['Wq'], 'L0_xattn_bq': _L0_xattn_in['bq'], 'L0_xattn_Wk': _L0_xattn_in['Wk'], 'L0_xattn_bk': _L0_xattn_in['bk'], 'L0_xattn_Wv': _L0_xattn_in['Wv'], 'L0_xattn_bv': _L0_xattn_in['bv'], 'L0_xattn_Wo': _L0_xattn_in['Wo'], 'L0_xattn_bo': _L0_xattn_in['bo'], 'L0_ffn_gate_w': _L0_ffn_in['gate_w'], 'L0_ffn_lora_A': _L0_ffn_in['lora_A'], 'L0_ffn_lora_B': _L0_ffn_in['lora_B']}

def reference(x, ctx_4096, L0_xattn_Wq, L0_xattn_bq, L0_xattn_Wk, L0_xattn_bk, L0_xattn_Wv, L0_xattn_bv, L0_xattn_Wo, L0_xattn_bo, L0_ffn_gate_w, L0_ffn_lora_A, L0_ffn_lora_B):
    import jax
    import jax.numpy as jnp

    def _L0_xattn_ref(x, cond, Wq, bq, Wk, bk, Wv, bv, Wo, bo):
        import jax, jax.numpy as jnp
        import numpy as np
        HEADS = 8
        WINDOW = 16

        def _pointwise(W, b, t):
            return jnp.einsum('oc,bct->bot', W, t) + b[None, :, None]
        B, C, T = x.shape
        H, W = (HEADS, WINDOW)
        hd = C // H
        scale = hd ** (-0.5)
        pad_left = W // 2
        pad_right = W - pad_left - 1
        q = _pointwise(Wq, bq, x)
        k = _pointwise(Wk, bk, cond)
        v = _pointwise(Wv, bv, cond)
        k = jnp.pad(k, ((0, 0), (0, 0), (pad_left, pad_right)))
        v = jnp.pad(v, ((0, 0), (0, 0), (pad_left, pad_right)))
        idx = jnp.arange(T)[:, None] + jnp.arange(W)[None, :]
        k_win = k[:, :, idx].reshape(B, H, hd, T, W)
        v_win = v[:, :, idx].reshape(B, H, hd, T, W)
        qh = q.reshape(B, H, hd, T)
        dots = jnp.einsum('bhdt,bhdtw->bhtw', qh, k_win) * scale
        attn = jax.nn.softmax(dots, axis=-1)
        out = jnp.einsum('bhtw,bhdtw->bhdt', attn, v_win)
        out = out.reshape(B, C, T)
        return _pointwise(Wo, bo, out)

    def _L0_ffn_ref(inputs, gate_w, lora_A, lora_B):
        import jax, jax.numpy as jnp
        import numpy as np
        N_EXPERTS = 8
        TOP_K = 2
        D_MODEL = 1024
        RANK = 64
        x = inputs.reshape(-1, inputs.shape[-1])
        T = x.shape[0]
        gate_probs = jax.nn.softmax(x @ gate_w.T, axis=-1)
        weights, sel = jax.lax.top_k(gate_probs, TOP_K)
        weights = weights / jnp.sum(weights, axis=-1, keepdims=True)
        w_full = jnp.zeros((T, N_EXPERTS), dtype=x.dtype).at[jnp.arange(T)[:, None], sel].add(weights)
        out = jnp.zeros((T, D_MODEL), dtype=x.dtype)
        for e in range(N_EXPERTS):
            y = x @ lora_A[e].T @ lora_B[e].T
            out = out + w_full[:, e:e + 1] * y
        return out.reshape(inputs.shape[:-1] + (D_MODEL,))
    x = x + _L0_xattn_ref(_layernorm(x, axis=-1), ctx_4096, L0_xattn_Wq, L0_xattn_bq, L0_xattn_Wk, L0_xattn_bk, L0_xattn_Wv, L0_xattn_bv, L0_xattn_Wo, L0_xattn_bo)
    x = x + _L0_ffn_ref(_layernorm(x, axis=-1), L0_ffn_gate_w, L0_ffn_lora_A, L0_ffn_lora_B)
    return x

_drawn_inputs = setup_inputs


def setup_inputs(seed=0):
    import zlib

    import numpy as np

    out = dict(_drawn_inputs(seed))
    spreads = {'L0_xattn_bq': (0.0, 0.8),
     'L0_xattn_bk': (0.0, 0.8),
     'L0_xattn_bv': (0.0, 0.356),
     'L0_xattn_bo': (0.0, 0.1)}
    factors = {'ctx_4096': 4.123, 'L0_xattn_Wq': 8.0, 'L0_xattn_Wk': 8.0, 'L0_xattn_Wv': 4.117}
    for name, (base, spread) in spreads.items():
        noise = np.random.default_rng([zlib.crc32(name.encode()), seed]).standard_normal(out[name].shape)
        drawn = base * np.exp(spread * noise) if base else spread * noise
        out[name] = jnp.asarray(drawn.astype(out[name].dtype))
    for name, factor in factors.items():
        out[name] = (out[name] * factor).astype(out[name].dtype)
    return out
```

```python
from contextlib import ExitStack

import numpy as np

import concourse.bass as bass
from concourse import mybir

F32 = mybir.dt.float32
F32R = mybir.dt.float32r
BF16 = mybir.dt.bfloat16
U32 = mybir.dt.uint32
ALU = mybir.AluOpType
ACT = mybir.ActivationFunctionType
AX_X = mybir.AxisListType.X

P = 128
T = 1024
BATCHES = 32
HEADS = 8
HD = P // HEADS
WINDOW = 16
PAD_LEFT = WINDOW // 2
QT = 16
KT = 32
TILES = T // QT
CHUNKS = 4
CT = TILES // CHUNKS
CW = CT * KT
GROUPS = 4
KPAD = T + 2 * PAD_LEFT
PAIRS = 4
PW = P // PAIRS
EXPERTS = 8
RANK = 64
ER = EXPERTS * RANK
FK = T // P
EK = ER // P
HALF = T // 2
ER2 = ER // 2
DW = ER + EXPERTS
D1 = ER2 + EXPERTS
EPS = 1e-5
SCALE = HD ** -0.5
MASKED = -1e30
MASK_AT = EK * T + 4 * P


class Batch:

    def __init__(self, j, c):
        self.j, self.c = j, c

    def count(self, per, k):
        fixed = per * self.c + k
        return fixed if isinstance(self.j, int) and self.j == 0 else self.j * (2 * per) + fixed

    def turn(self, k):
        fixed = 16 * (self.c // 2 + k)
        return fixed if isinstance(self.j, int) and self.j == 0 else self.j * 16 + fixed

    @property
    def parity(self):
        return self.c % 2

    def row(self, eng):
        return self.c if isinstance(self.j, int) and self.j == 0 else eng.snap(self.j * 2 + self.c)


def build(nc, x, ctx, wqkvo, biases, down_w, up_w, ident_in, masks_in, consts_in, out):
    with ExitStack() as stack:
        def sb(name, shape, dt=F32):
            return stack.enter_context(nc.sbuf_tensor(name, shape, dt))

        def psum(name, cols):
            return stack.enter_context(nc.psum_tensor(name, [P, cols], F32))

        def sem(name):
            return stack.enter_context(nc.semaphore(name))

        w_split = sb("w_split", [P, 2, 4 * P], F32R)
        down_split = sb("down_split", [P, 2, FK * DW], F32R)
        up_split = sb("up_split", [P, 2, EK * T], F32R)
        ident = sb("ident", [P, P])
        mask_rows = sb("mask_rows", [P, P], BF16)
        mask_cols = sb("mask_cols", [P, CW], BF16)
        bias = sb("bias", [P, 4])
        bq_scaled = sb("bq_scaled", [P, 1])
        consts = sb("consts", [P, 4 + EXPERTS])
        q_diag = sb("q_diag", [P, HEADS * T])
        v_diag = sb("v_diag", [P, PAIRS * PW * TILES])
        raw = sb("raw", [P, T])
        src_split = sb("src_split", [P, 2, T], F32R)
        resid = [sb(f"resid{n}", [P, T]) for n in range(2)]
        q_sb = sb("q_sb", [P, T])
        k_sb = sb("k_sb", [P, KPAD])
        v_sb = sb("v_sb", [P, KPAD])
        v_t = sb("v_t", [P, PW * TILES])
        prob = sb("prob", [P, 2, CW])
        prob_t = sb("prob_t", [P, TILES * KT])
        attn = sb("attn", [P, T])
        mid_split = sb("mid_split", [P, 2, T], F32R)
        h_sb = sb("h_sb", [P, ER])
        ht_split = sb("ht_split", [P, 2, ER], F32R)
        row_max = sb("row_max", [P, TILES])
        row_sum = sb("row_sum", [P, TILES])
        row_inv = sb("row_inv", [P, TILES])
        stats = sb("stats", [P, 2, 2, 6])
        moments = sb("moments", [P, 2, 2])
        var_eps = sb("var_eps", [P, 2])
        rstd = sb("rstd", [P, 2])
        shift = sb("shift", [P, 2])
        logits = sb("logits", [P, EXPERTS])
        top = sb("top", [P, 8])
        top_at = sb("top_at", [P, 8], U32)
        top_atf = sb("top_atf", [P, 2])
        gate = sb("gate", [P, 5])
        fences = sb("fences", [P, 3])
        pick = sb("pick", [P, 3, EXPERTS])

        bank_a = psum("bank_a", T)
        bank_b = [psum(f"bank_b{m}", CW) for m in range(CHUNKS)]
        bank_c = psum("bank_c", T)

        down_in, up_in, small_in = sem("down_in"), sem("up_in"), sem("small_in")
        weights_split, masks_ready, bq_ready = sem("weights_split"), sem("masks_ready"), sem("bq_ready")
        pads_zero, q_diag_rest = sem("pads_zero"), sem("q_diag_rest")
        q_diag_zero, v_diag_zero = sem("q_diag_zero"), sem("v_diag_zero")
        raw_in = sem("raw_in")
        resid_in = [sem("resid_in0"), sem("resid_in1")]
        stored = [sem("stored0"), sem("stored1")]
        q_placed, v_placed = sem("q_placed"), sem("v_placed")
        q_done, k_done, v_done = sem("q_done"), sem("k_done"), sem("v_done")
        down_done, pv_done, ht_done = sem("down_done"), sem("pv_done"), sem("ht_done")
        scores_done, o_done = sem("scores_done"), sem("o_done")
        up_done, xt_done = sem("up_done"), sem("xt_done")
        q_out, k_out, v_out = sem("q_out"), sem("k_out"), sem("v_out")
        gap_exp, even_out, ht_hi = sem("gap_exp"), sem("even_out"), sem("ht_hi")
        exp_done, xt_hi = sem("exp_done"), sem("xt_hi")
        v_t_done, gate_step, h_done = sem("v_t_done"), sem("gate_step"), sem("h_done")
        attn_done, attn_hi = sem("attn_done"), sem("attn_hi")
        ln1_step, xn_done, xn_hi = sem("ln1_step"), sem("xn_done"), sem("xn_hi")
        ht_lo, max_done, shifted = sem("ht_lo"), sem("max_done"), sem("shifted")
        sum_done, inv_done, prob_t_done = sem("sum_done"), sem("inv_done"), sem("prob_t_done")
        x1_done, ln2_step, xn2_done = sem("x1_done"), sem("ln2_step"), sem("xn2_done")
        ctx_hi, result_done, xt_lo = sem("ctx_hi"), sem("result_done"), sem("xt_lo")
        attn_lo, rstd1, xn_lo = sem("attn_lo"), sem("rstd1"), sem("xn_lo")
        prob_done, rstd2, ctx_lo = sem("prob_done"), sem("rstd2"), sem("ctx_lo")

        block = stack.enter_context(nc.Block())

        def steps(eng, step):
            lead, tail = 4, 3
            loops = (BATCHES + 3 - lead - tail) // 2
            first = lead - 1
            for i in range(-1, first):
                step(*(Batch(0, i + d) if 0 <= i + d < BATCHES else None for d in (1, 0, -1, -2)))
            with eng.Fori(0, loops) as j:
                for u in range(2):
                    step(*(Batch(j, first + u + d) for d in (1, 0, -1, -2)))
            for i in range(first + 2 * loops, BATCHES + 2):
                step(*(Batch(0, i + d) if 0 <= i + d < BATCHES else None for d in (1, 0, -1, -2)))

        @block.sync
        def _(sp):
            sp.dma_start(v_diag[:, 0:FK * DW], down_w).then_inc(down_in, 16)
            sp.dma_start(q_diag[:, 0:EK * T], up_w).then_inc(up_in, 16)
            sp.dma_start(q_diag[:, EK * T:EK * T + 4 * P], wqkvo).then_inc(small_in, 16)
            sp.dma_start(q_diag[:, MASK_AT:MASK_AT + P + CW], masks_in).then_inc(small_in, 16)
            sp.dma_start(bias[:], biases).then_inc(small_in, 16)
            sp.dma_start(ident[:], ident_in).then_inc(small_in, 16)
            sp.dma_start(consts[:], consts_in).then_inc(small_in, 16)

            def step(ahead, cur, prev, old):
                ahead_row, prev_row, old_row = (b and b.row(sp) for b in (ahead, prev, old))
                if ahead:
                    if ahead.c >= 1:
                        sp.wait_ge(ctx_lo, ahead.count(1, 0))
                    sp.dma_start(raw[:], x[ahead_row]).then_inc(raw_in, 16)
                if prev:
                    if prev.c >= 2:
                        sp.wait_ge(stored[prev.parity], prev.turn(0))
                    sp.dma_start(resid[prev.parity][:], x[prev_row]).then_inc(resid_in[prev.parity], 16)
                if ahead:
                    sp.wait_ge(xn_lo, ahead.count(1, 1))
                    sp.dma_start(raw[:], ctx[ahead_row]).then_inc(raw_in, 16)
                if cur:
                    if cur.c >= 1:
                        sp.wait_ge(pv_done, cur.count(CHUNKS, 0))
                    else:
                        sp.wait_ge(v_diag_zero, 1)
                    sp.wait_ge(v_t_done, cur.count(1, 1))
                    for g in range(PAIRS):
                        sp.dma_start(v_diag[PW * g:PW * (g + 1), g * PW * TILES:(g + 1) * PW * TILES],
                                     v_t[PW * g:PW * (g + 1), :]).then_inc(v_placed, 16)
                if ahead:
                    if ahead.c >= 1:
                        sp.wait_ge(scores_done, ahead.count(CHUNKS, 0))
                    else:
                        sp.wait_ge(q_diag_zero, 1)
                        sp.wait_ge(q_diag_rest, 1)
                    sp.wait_ge(q_out, ahead.count(1, 1))
                    for h in range(HEADS):
                        sp.dma_start(q_diag[HD * h:HD * (h + 1), h * T:(h + 1) * T],
                                     q_sb[HD * h:HD * (h + 1), :]).then_inc(q_placed, 16)
                if old:
                    sp.wait_ge(result_done, old.count(2, 2))
                    sp.dma_start(out[old_row], resid[old.parity][:]).then_inc(stored[old.parity], 16)

            steps(sp, step)
            sp.wait_ge(stored[0], 16 * (BATCHES // 2))
            sp.wait_ge(stored[1], 16 * (BATCHES // 2))

        @block.tensor
        def _(pe):
            pe.wait_ge(weights_split, 6)
            pe.wait_ge(masks_ready, 2)
            pe.wait_ge(pads_zero, 2)

            def one_pass(n, dst, st, st_cols, mv, mv_cols, start, stop):
                s, m = ((0, 0), (0, 1), (1, 0))[n]
                return nc.tensor.matmul(dst, st[:, s, st_cols], mv[:, m, mv_cols],
                                        start=start and n == 0, stop=stop and n == 2)

            def product(*operands):
                for n in range(3):
                    last = one_pass(n, *operands)
                return last

            def project_pass(n, bank, which, source):
                half = slice(n // 3 * HALF, (n // 3 + 1) * HALF)
                return one_pass(n % 3, bank[:, half], w_split, slice(which * P, (which + 1) * P),
                                source, half, True, True)

            def step(ahead, cur, prev, old):
                if cur:
                    pe.wait_ge(ctx_hi, cur.count(1, 1))
                    pe.wait_ge(ctx_lo, cur.count(1, 1))
                    if cur.c >= 2:
                        pe.wait_ge(x1_done, cur.count(2, -2))
                    pe.wait_ge(q_out, cur.count(1, 1))
                    for n in range(6):
                        last = project_pass(n, bank_c, 2, src_split)
                    last.then_inc(v_done, 1)
                    for n in range(6):
                        if n % 3 == 0 and cur.c >= 3:
                            pe.wait_ge(result_done, cur.count(2, n // 3 - 5))
                        last = project_pass(n, bank_a, 1, src_split)
                    last.then_inc(k_done, 1)
                if old:
                    pe.wait_ge(xt_hi, old.count(2, 2))
                    pe.wait_ge(xt_lo, old.count(2, 2))
                    if prev:
                        pe.wait_ge(shifted, prev.count(CHUNKS, CHUNKS))
                if prev:
                    pe.wait_ge(v_placed, prev.count(16 * PAIRS, 16 * PAIRS))
                for m in range(CHUNKS):
                    if prev:
                        pe.wait_ge(prob_t_done, prev.count(CHUNKS, m + 1))
                        if m >= 2:
                            pe.wait_ge(attn_done, prev.count(CHUNKS, m - 1))
                        elif prev.c >= 1:
                            pe.wait_ge(xt_lo, prev.count(2, m - 1))
                    for s in range(GROUPS):
                        if prev:
                            for t in range(s * CT // GROUPS, (s + 1) * CT // GROUPS):
                                n = m * CT + t
                                last = nc.tensor.matmul(
                                    bank_b[m % 2][:, t * PW:(t + 1) * PW],
                                    v_diag[:, n:n + (P - 1) * TILES + 1:TILES],
                                    prob_t[:, n * KT:(n + 1) * KT], start=True, stop=True)
                            if s == GROUPS - 1:
                                last.then_inc(pv_done, 1)
                        if old:
                            n, f = divmod(m * GROUPS + s, FK)
                            lo, hi = ((0, D1), (D1, DW))[n]
                            last = product(bank_b[2 + n][:, 0:hi - lo], mid_split,
                                           slice(f * P, (f + 1) * P), down_split,
                                           slice(f * DW + lo, f * DW + hi), f == 0, f == FK - 1)
                            if f == FK - 1:
                                last.then_inc(down_done, 1)
                if ahead:
                    pe.wait_ge(xn_hi, ahead.count(1, 1))
                    pe.wait_ge(xn_lo, ahead.count(1, 1))
                    if cur:
                        pe.wait_ge(v_out, cur.count(1, 1))
                if cur:
                    pe.wait_ge(q_placed, cur.count(16 * HEADS, 16 * HEADS))
                    pe.wait_ge(k_out, cur.count(1, 1))
                for m in range(CHUNKS):
                    if m == 1 and old:
                        pe.wait_ge(h_done, old.count(2, 2))
                        if cur:
                            pe.wait_ge(k_out, cur.count(1, 1))
                        else:
                            pe.wait_ge(result_done, old.count(2, 0))
                        for e in range(EK):
                            last = nc.tensor.transpose(bank_a[:, e * P:(e + 1) * P],
                                                       h_sb[:, e * P:(e + 1) * P], ident[:])
                        last.then_inc(ht_done, 1)
                    if m == 1 and prev:
                        pe.wait_ge(attn_hi, prev.count(1, 1))
                        pe.wait_ge(attn_lo, prev.count(1, 1))
                    if m == 3 and prev:
                        pe.wait_ge(xn2_done, prev.count(1, 1))
                        if cur:
                            pe.wait_ge(shifted, cur.count(CHUNKS, 2))
                        for f in range(FK):
                            last = nc.tensor.transpose(bank_b[f // 4][:, f % 4 * P:(f % 4 + 1) * P],
                                                       attn[:, f * P:(f + 1) * P], ident[:])
                            if f % 4 == 3:
                                last.then_inc(xt_done, 1)
                    if m == 2 and old:
                        pe.wait_ge(ht_hi, old.count(1, 1))
                        pe.wait_ge(ht_lo, old.count(1, 1))
                    if cur:
                        if m >= 2 and old:
                            pe.wait_ge(h_done, old.count(2, m - 1))
                        if m < 2 and cur.c >= 1:
                            pe.wait_ge(attn_done, cur.count(CHUNKS, m - 1))
                        nc.tensor.matmul(bank_b[m][:], mask_rows[:], mask_cols[:],
                                         start=True, stop=False, skip_group_check=True)
                    for s in range(GROUPS):
                        if cur:
                            for t in range(s * CT // GROUPS, (s + 1) * CT // GROUPS):
                                n = m * CT + t
                                last = nc.tensor.matmul(
                                    bank_b[m][:, t * KT:(t + 1) * KT],
                                    q_diag[:, n:n + (P - 1) * TILES + 1:TILES],
                                    k_sb[:, n * QT:n * QT + KT],
                                    start=False, stop=t == CT - 1, skip_group_check=True)
                            if s == GROUPS - 1:
                                last.then_inc(scores_done, 1)
                        passes = ((0, 1), (2,), (3, 4), (5,))[s]
                        if m == 0 and ahead:
                            for n in passes:
                                last = project_pass(n, bank_c, 0, src_split)
                            if s == GROUPS - 1:
                                last.then_inc(q_done, 1)
                        if m == 1 and prev:
                            if s == 0 and ahead:
                                pe.wait_ge(q_out, ahead.count(1, 1))
                            for n in passes:
                                last = project_pass(n, bank_c, 3, mid_split)
                                if n % 3 == 2:
                                    last.then_inc(o_done, 1)
                        if m >= 2 and old:
                            n, e = m - 2, s
                            last = product(bank_a[:, n * HALF:(n + 1) * HALF], ht_split,
                                           slice(e * P, (e + 1) * P), up_split,
                                           slice(e * T + n * HALF, e * T + (n + 1) * HALF),
                                           e == 0, e == EK - 1)
                            if e == EK - 1:
                                last.then_inc(up_done, 1)

            steps(pe, step)

        @block.scalar
        def _(act):
            act.wait_ge(pads_zero, 2)
            act.wait_ge(small_in, 16 * 5)

            def even_heads(prev, m):
                act.wait_ge(pv_done, prev.count(CHUNKS, m + 1))
                if m == 0 and prev.c >= 1:
                    act.wait_ge(xt_done, prev.count(2, 0))
                src = bank_b[m % 2][:].rearrange("p (n h i) -> p n h i", h=2, i=QT)
                dst = attn[:, m * CT * QT:(m + 1) * CT * QT]
                nc.scalar.activation(dst.rearrange("p (n i) -> p n i", i=QT), src[:, :, 0, :],
                                     ACT.Copy, scale=consts[:, 0:1]).then_inc(even_out, 1)

            def exponentials(cur, m):
                act.wait_ge(shifted, cur.count(CHUNKS, m + 1))
                nc.scalar.activation(prob[:, m % 2, :], prob[:, m % 2, :], ACT.Exp).then_inc(exp_done, 1)

            def step(ahead, cur, prev, old):
                if cur:
                    act.wait_ge(v_done, cur.count(1, 1))
                    if cur.c >= 1:
                        act.wait_ge(v_t_done, cur.count(1, 0))
                    nc.scalar.activation(v_sb[:, PAD_LEFT:PAD_LEFT + T], bank_c[:], ACT.Identity,
                                         bias=bias[:, 2:3]).then_inc(v_out, 1)
                    act.wait_ge(k_done, cur.count(1, 1))
                    if cur.c >= 1:
                        act.wait_ge(scores_done, cur.count(CHUNKS, 0))
                    nc.scalar.activation(k_sb[:, PAD_LEFT:PAD_LEFT + T], bank_a[:], ACT.Identity,
                                         bias=bias[:, 1:2]).then_inc(k_out, 1)
                if prev:
                    even_heads(prev, 0)
                    even_heads(prev, 1)
                if old:
                    act.wait_ge(gate_step, old.count(13, 7))
                    nc.scalar.activation(gate[:, 1:2], gate[:, 0:1], ACT.Exp).then_inc(gap_exp, 1)
                if prev:
                    even_heads(prev, 2)
                    even_heads(prev, 3)
                if ahead:
                    act.wait_ge(q_done, ahead.count(1, 1))
                    if ahead.c >= 1:
                        act.wait_ge(q_placed, ahead.count(16 * HEADS, 0))
                    else:
                        act.wait_ge(bq_ready, 1)
                    nc.scalar.activation(q_sb[:].rearrange("p (i n) -> p n i", n=TILES),
                                         bank_c[:].rearrange("p (n i) -> p n i", i=QT), ACT.Identity,
                                         bias=bq_scaled[:], scale=SCALE).then_inc(q_out, 1)
                if cur:
                    exponentials(cur, 0)
                if old:
                    act.wait_ge(ht_done, old.count(1, 1))
                    if old.c >= 1:
                        act.wait_ge(up_done, old.count(2, 0))
                    nc.scalar.activation(ht_split[:, 0, :], bank_a[:, 0:ER], ACT.Copy).then_inc(ht_hi, 1)
                if cur:
                    exponentials(cur, 1)
                    exponentials(cur, 2)
                if prev:
                    for n in range(2):
                        act.wait_ge(xt_done, prev.count(2, n + 1))
                        nc.scalar.activation(mid_split[:, 0, n * HALF:(n + 1) * HALF], bank_b[n][:],
                                             ACT.Copy).then_inc(xt_hi, 1)
                if cur:
                    exponentials(cur, 3)

            steps(act, step)

        @block.vector
        def _(dve):
            def split(which, parts, src):
                nc.vector.tensor_copy(parts[:, 0, :], src).then_inc(weights_split, 1)
                dve.wait_ge(weights_split, 2 * which + 1)
                nc.vector.tensor_tensor(parts[:, 1, :], src, parts[:, 0, :].bitcast(F32),
                                        ALU.subtract).then_inc(weights_split, 1)

            dve.wait_ge(down_in, 16)
            split(0, down_split, v_diag[:, 0:FK * DW])
            dve.wait_ge(up_in, 16)
            split(1, up_split, q_diag[:, 0:EK * T])
            dve.wait_ge(small_in, 16 * 5)
            split(2, w_split, q_diag[:, EK * T:EK * T + 4 * P])
            nc.vector.tensor_copy(mask_rows[:], q_diag[:, MASK_AT:MASK_AT + P]).then_inc(masks_ready, 1)
            nc.vector.tensor_copy(mask_cols[:], q_diag[:, MASK_AT + P:MASK_AT + P + CW]).then_inc(masks_ready, 1)
            nc.vector.tensor_scalar(bq_scaled[:], bias[:, 0:1], SCALE, None, ALU.mult).then_inc(bq_ready, 1)
            dve.wait_ge(weights_split, 6)
            dve.wait_ge(masks_ready, 2)
            nc.vector.memset(q_diag[:, 0:MASK_AT + P + CW], 0.0).then_inc(q_diag_zero, 1)

            def fence(semaphore, which):
                nc.vector.memset(fences[:, which:which + 1], 0.0).then_inc(semaphore, 1)

            def layernorm_stats(which, source, semaphore, batch):
                for n in range(2):
                    nc.vector.bn_stats(stats[:, which, n, :],
                                       source[:, n * HALF:(n + 1) * HALF]).then_inc(semaphore, 1)
                dve.wait_ge(semaphore, batch.count(6, 2))
                fence(semaphore, which)
                nc.vector.bn_aggr(moments[:, which, :],
                                  stats[:, which, :, :].rearrange("p a b -> p (a b)")).then_inc(semaphore, 1)
                dve.wait_ge(semaphore, batch.count(6, 4))
                nc.vector.tensor_scalar(var_eps[:, which:which + 1], moments[:, which, 1:2], EPS, None,
                                        ALU.add).then_inc(semaphore, 1)

            def layernorm_shift(which, semaphore, batch):
                nc.vector.scalar_tensor_tensor(shift[:, which:which + 1], moments[:, which, 0:1], -1.0,
                                               rstd[:, which:which + 1], ALU.mult,
                                               ALU.mult).then_inc(semaphore, 1)
                dve.wait_ge(semaphore, batch.count(6, 6))

            def join_heads(prev, m):
                dve.wait_ge(even_out, prev.count(CHUNKS, m + 1))
                src = bank_b[m % 2][:].rearrange("p (n h i) -> p n h i", h=2, i=QT)
                dst = attn[:, m * CT * QT:(m + 1) * CT * QT].rearrange("p (n i) -> p n i", i=QT)
                nc.vector.scalar_tensor_tensor(dst, src[:, :, 1, :], consts[:, 1:2], dst,
                                               ALU.mult, ALU.add).then_inc(attn_done, 1)

            def choose_experts(old):
                dve.wait_ge(down_done, old.count(2, 1))
                nc.vector.tensor_copy(logits[:], bank_b[2][:, ER2:D1]).then_inc(gate_step, 1)
                dve.wait_ge(gate_step, old.count(13, 1))
                fence(gate_step, 2)
                nc.vector.max(top[:], logits[:]).then_inc(gate_step, 1)
                dve.wait_ge(gate_step, old.count(13, 3))
                fence(gate_step, 2)
                nc.vector.max_index(top_at[:], top[:], logits[:]).then_inc(gate_step, 1)
                dve.wait_ge(gate_step, old.count(13, 5))
                nc.vector.tensor_copy(top_atf[:], top_at[:, 0:2]).then_inc(gate_step, 1)
                nc.vector.tensor_tensor(gate[:, 0:1], top[:, 1:2], top[:, 0:1],
                                        ALU.subtract).then_inc(gate_step, 1)
                dve.wait_ge(gap_exp, old.count(1, 1))
                nc.vector.tensor_scalar(gate[:, 2:3], gate[:, 1:2], 1.0, None, ALU.add).then_inc(gate_step, 1)
                dve.wait_ge(gate_step, old.count(13, 8))
                nc.vector.reciprocal(gate[:, 3:4], gate[:, 2:3]).then_inc(gate_step, 1)
                dve.wait_ge(gate_step, old.count(13, 9))
                nc.vector.tensor_tensor(gate[:, 4:5], gate[:, 1:2], gate[:, 3:4], ALU.mult).then_inc(gate_step, 1)
                dve.wait_ge(gate_step, old.count(13, 10))
                for n in range(2):
                    nc.vector.tensor_scalar(pick[:, n, :], consts[:, 4:4 + EXPERTS],
                                            top_atf[:, n:n + 1], gate[:, 3 + n:4 + n],
                                            ALU.is_equal, ALU.mult).then_inc(gate_step, 1)
                dve.wait_ge(gate_step, old.count(13, 12))
                nc.vector.tensor_tensor(pick[:, 2, :], pick[:, 0, :], pick[:, 1, :],
                                        ALU.add).then_inc(gate_step, 1)
                dve.wait_ge(gate_step, old.count(13, 13))

            def weigh_experts(old, n):
                experts = slice(n * EXPERTS // 2, (n + 1) * EXPERTS // 2)
                dve.wait_ge(down_done, old.count(2, n + 1))
                if n == 0 and old.c >= 1:
                    dve.wait_ge(ht_done, old.count(1, 0))
                nc.vector.tensor_tensor(
                    h_sb[:, n * ER2:(n + 1) * ER2].rearrange("p (e r) -> p e r", r=RANK),
                    bank_b[2 + n][:, 0:ER2].rearrange("p (e r) -> p e r", r=RANK),
                    pick[:, 2, experts].unsqueeze(2).broadcast_to([P, EXPERTS // 2, RANK]),
                    ALU.mult).then_inc(h_done, 1)

            def scores_shift(cur, m):
                cols = slice(m * CT, (m + 1) * CT)
                scores = bank_b[m][:].rearrange("p (n j) -> p n j", j=KT)
                dve.wait_ge(scores_done, cur.count(CHUNKS, m + 1))
                nc.vector.tensor_reduce(row_max[:, cols], scores, AX_X, ALU.max).then_inc(max_done, 1)
                dve.wait_ge(max_done, cur.count(CHUNKS, m + 1))
                if m >= 2 or cur.c >= 1:
                    dve.wait_ge(prob_t_done, cur.count(CHUNKS, m - 1))
                nc.vector.tensor_tensor(prob[:, m % 2, :].rearrange("p (n j) -> p n j", j=KT), scores,
                                        row_max[:, cols].unsqueeze(2).broadcast_to([P, CT, KT]),
                                        ALU.subtract).then_inc(shifted, 1)

            def weights_sum(cur, m):
                cols = slice(m * CT, (m + 1) * CT)
                dve.wait_ge(exp_done, cur.count(CHUNKS, m + 1))
                nc.vector.tensor_reduce(row_sum[:, cols],
                                        prob[:, m % 2, :].rearrange("p (n j) -> p n j", j=KT),
                                        AX_X, ALU.add).then_inc(sum_done, 1)
                dve.wait_ge(sum_done, cur.count(CHUNKS, m + 1))
                if m == 0 and cur.c >= 1:
                    dve.wait_ge(prob_done, cur.count(CHUNKS, 0))
                nc.vector.reciprocal(row_inv[:, cols], row_sum[:, cols]).then_inc(inv_done, 1)

            def weights_transpose(cur, m):
                dve.wait_ge(prob_done, cur.count(CHUNKS, m + 1))
                if m == 0 and cur.c >= 1:
                    dve.wait_ge(pv_done, cur.count(CHUNKS, 0))
                nc.vector.transpose(prob_t[:, m * CW:(m + 1) * CW],
                                    prob[:, m % 2, :]).then_inc(prob_t_done, 1)

            def add_mixture(old, n):
                y = resid[old.parity][:, n * HALF:(n + 1) * HALF]
                dve.wait_ge(up_done, old.count(2, n + 1))
                nc.vector.tensor_tensor(y, bank_a[:, n * HALF:(n + 1) * HALF], y,
                                        ALU.add).then_inc(result_done, 1)

            def step(ahead, cur, prev, old):
                if cur:
                    dve.wait_ge(v_out, cur.count(1, 1))
                    if cur.c >= 1:
                        dve.wait_ge(v_placed, cur.count(16 * PAIRS, 0))
                    windows = bass.AP(tensor=v_sb[:].tensor, offset=0,
                                      ap=[[KPAD, P], [QT, TILES], [1, KT]])
                    nc.vector.transpose(v_t[:].rearrange("p (c n) -> p n c", n=TILES),
                                        windows).then_inc(v_t_done, 1)
                if ahead:
                    dve.wait_ge(raw_in, ahead.count(32, 16))
                    layernorm_stats(0, raw, ln1_step, ahead)
                if prev:
                    join_heads(prev, 0)
                if ahead:
                    dve.wait_ge(rstd1, ahead.count(1, 1))
                    layernorm_shift(0, ln1_step, ahead)
                    nc.vector.tensor_scalar(raw[:], raw[:], rstd[:, 0:1], shift[:, 0:1], ALU.mult,
                                            ALU.add).then_inc(xn_done, 1)
                    dve.wait_ge(xn_done, ahead.count(1, 1))
                    if cur:
                        dve.wait_ge(k_done, cur.count(1, 1))
                    nc.vector.tensor_copy(src_split[:, 0, :], raw[:]).then_inc(xn_hi, 1)
                if prev:
                    join_heads(prev, 1)
                if old:
                    choose_experts(old)
                    weigh_experts(old, 0)
                if prev:
                    join_heads(prev, 2)
                    join_heads(prev, 3)
                if old:
                    weigh_experts(old, 1)
                if prev:
                    dve.wait_ge(attn_done, prev.count(CHUNKS, CHUNKS))
                    if old:
                        dve.wait_ge(down_done, old.count(2, 2))
                    nc.vector.tensor_copy(mid_split[:, 0, :], attn[:]).then_inc(attn_hi, 1)
                if cur:
                    scores_shift(cur, 0)
                if old:
                    dve.wait_ge(ht_hi, old.count(1, 1))
                    nc.vector.tensor_tensor(ht_split[:, 1, :], bank_a[:, 0:ER],
                                            ht_split[:, 0, :].bitcast(F32),
                                            ALU.subtract).then_inc(ht_lo, 1)
                if cur:
                    weights_sum(cur, 0)
                    scores_shift(cur, 1)
                if prev:
                    x1 = resid[prev.parity]
                    dve.wait_ge(resid_in[prev.parity], prev.turn(1))
                    for n in range(2):
                        half = slice(n * HALF, (n + 1) * HALF)
                        dve.wait_ge(o_done, prev.count(2, n + 1))
                        nc.vector.scalar_tensor_tensor(x1[:, half], bank_c[:, half], bias[:, 3:4],
                                                       x1[:, half], ALU.add,
                                                       ALU.add).then_inc(x1_done, 1)
                    dve.wait_ge(x1_done, prev.count(2, 2))
                    layernorm_stats(1, x1, ln2_step, prev)
                if cur:
                    weights_transpose(cur, 0)
                    weights_sum(cur, 1)
                if ahead:
                    dve.wait_ge(raw_in, ahead.count(32, 32))
                    dve.wait_ge(q_done, ahead.count(1, 1))
                    nc.vector.tensor_copy(src_split[:, 0, :], raw[:]).then_inc(ctx_hi, 1)
                if prev:
                    dve.wait_ge(rstd2, prev.count(1, 1))
                    layernorm_shift(1, ln2_step, prev)
                    dve.wait_ge(attn_lo, prev.count(1, 1))
                    nc.vector.tensor_scalar(attn[:], x1[:], rstd[:, 1:2], shift[:, 1:2], ALU.mult,
                                            ALU.add).then_inc(xn2_done, 1)
                if cur:
                    weights_transpose(cur, 1)
                    scores_shift(cur, 2)
                    weights_sum(cur, 2)
                if prev:
                    for n in range(2):
                        half = slice(n * HALF, (n + 1) * HALF)
                        dve.wait_ge(xt_hi, prev.count(2, n + 1))
                        nc.vector.tensor_tensor(mid_split[:, 1, half], bank_b[n][:],
                                                mid_split[:, 0, half].bitcast(F32),
                                                ALU.subtract).then_inc(xt_lo, 1)
                if old:
                    add_mixture(old, 0)
                if cur:
                    scores_shift(cur, 3)
                if old:
                    add_mixture(old, 1)
                if cur:
                    weights_sum(cur, 3)
                    weights_transpose(cur, 2)
                    weights_transpose(cur, 3)

            steps(dve, step)

        @block.gpsimd
        def _(pool):
            nc.gpsimd.memset(k_sb[:], 0.0).then_inc(pads_zero, 1)
            nc.gpsimd.memset(v_sb[:], 0.0).then_inc(pads_zero, 1)
            nc.gpsimd.memset(q_diag[:, MASK_AT + P + CW:], 0.0).then_inc(q_diag_rest, 1)
            pool.wait_ge(weights_split, 2)
            nc.gpsimd.memset(v_diag[:], 0.0).then_inc(v_diag_zero, 1)
            pool.wait_ge(small_in, 16 * 5)

            def weights_norm(cur, m):
                cols = slice(m * CT, (m + 1) * CT)
                pool.wait_ge(inv_done, cur.count(CHUNKS, m + 1))
                p3 = prob[:, m % 2, :].rearrange("p (n j) -> p n j", j=KT)
                nc.gpsimd.tensor_tensor(p3, p3, row_inv[:, cols].unsqueeze(2).broadcast_to([P, CT, KT]),
                                        ALU.mult).then_inc(prob_done, 1)

            def step(ahead, cur, prev, old):
                if ahead:
                    pool.wait_ge(ln1_step, ahead.count(6, 5))
                    nc.gpsimd.tensor_tensor(rstd[:, 0:1], var_eps[:, 0:1], consts[:, 2:3],
                                            ALU.pow).then_inc(rstd1, 1)
                    pool.wait_ge(xn_hi, ahead.count(1, 1))
                    nc.gpsimd.tensor_tensor(src_split[:, 1, :], raw[:], src_split[:, 0, :].bitcast(F32),
                                            ALU.subtract).then_inc(xn_lo, 1)
                if prev:
                    pool.wait_ge(attn_hi, prev.count(1, 1))
                    nc.gpsimd.tensor_tensor(mid_split[:, 1, :], attn[:], mid_split[:, 0, :].bitcast(F32),
                                            ALU.subtract).then_inc(attn_lo, 1)
                if cur:
                    weights_norm(cur, 0)
                if prev:
                    pool.wait_ge(ln2_step, prev.count(6, 5))
                    nc.gpsimd.tensor_tensor(rstd[:, 1:2], var_eps[:, 1:2], consts[:, 2:3],
                                            ALU.pow).then_inc(rstd2, 1)
                if cur:
                    weights_norm(cur, 1)
                if ahead:
                    pool.wait_ge(ctx_hi, ahead.count(1, 1))
                    nc.gpsimd.tensor_tensor(src_split[:, 1, :], raw[:], src_split[:, 0, :].bitcast(F32),
                                            ALU.subtract).then_inc(ctx_lo, 1)
                if cur:
                    weights_norm(cur, 2)
                    weights_norm(cur, 3)

            steps(pool, step)


def shape_constants():
    rows = np.arange(P)
    mask_rows = (rows[:, None] == rows[None, :] % QT).astype(np.float32)
    key = np.arange(CW) % KT
    inside = (key[None, :] >= rows[:, None]) & (key[None, :] < rows[:, None] + WINDOW)
    mask_cols = np.where(inside | (rows[:, None] >= QT), 0.0, MASKED).astype(np.float32)
    consts = np.zeros((P, 4 + EXPERTS), np.float32)
    consts[:, 0] = rows // HD % 2 == 0
    consts[:, 1] = rows // HD % 2 == 1
    consts[:, 2] = -0.5
    consts[:, 3] = EPS
    consts[:, 4:] = np.arange(EXPERTS)
    return np.eye(P, dtype=np.float32), np.concatenate([mask_rows, mask_cols], axis=1), consts


def kernel(**inputs):
    import numpy as np
    import concourse.bacc as bacc
    from concourse import mybir
    from concourse.bass_utils import run_bass_kernel_spmd

    a = {k: np.asarray(v) for k, v in inputs.items()}
    x, ctx = a["x"], a["ctx_4096"]
    wqkvo = np.concatenate([a[f"L0_xattn_W{n}"].T for n in "qkvo"], axis=1)
    biases = np.stack([a[f"L0_xattn_b{n}"] for n in "qkvo"], axis=1)
    down = a["L0_ffn_lora_A"].reshape(ER, T)
    down = np.concatenate([down[:ER2], a["L0_ffn_gate_w"], down[ER2:]], axis=0)
    down = down.T.reshape(FK, P, DW).transpose(1, 0, 2).reshape(P, FK * DW)
    up = a["L0_ffn_lora_B"].transpose(0, 2, 1).reshape(EK, P, T).transpose(1, 0, 2).reshape(P, EK * T)
    ident, masks, consts = shape_constants()

    arrays = {
        "x": x, "ctx": ctx, "wqkvo": wqkvo, "biases": biases, "down_w": down, "up_w": up,
        "ident_in": ident, "masks_in": masks, "consts_in": consts,
    }
    arrays = {k: np.ascontiguousarray(v) for k, v in arrays.items()}
    nc = bacc.Bacc("TRN2", target_bir_lowering=False, num_devices=1)
    args = [nc.dram_tensor(k, v.shape, mybir.dt.from_np(v.dtype), kind="ExternalInput").ap()
            for k, v in arrays.items()]
    out = nc.dram_tensor("out", x.shape, mybir.dt.float32, kind="ExternalOutput").ap()
    build(nc, *args, out)
    r = run_bass_kernel_spmd(nc, [arrays], core_ids=[0])
    return r.results[0]["out"]
```

```python
from contextlib import ExitStack

import numpy as np

import concourse.bass as bass
from concourse import mybir

F32 = mybir.dt.float32
F32R = mybir.dt.float32r
BF16 = mybir.dt.bfloat16
U32 = mybir.dt.uint32
ALU = mybir.AluOpType
ACT = mybir.ActivationFunctionType
AX_X = mybir.AxisListType.X

P = 128
T = 1024
BATCHES = 32
HEADS = 8
HD = P // HEADS
WINDOW = 16
PAD_LEFT = WINDOW // 2
QT = 16
KT = 32
TILES = T // QT
CHUNKS = 4
CT = TILES // CHUNKS
CW = CT * KT
HT = TILES // 2
GROUPS = 4
KPAD = T + 2 * PAD_LEFT
PAIRS = 4
PW = P // PAIRS
EXPERTS = 8
RANK = 64
ER = EXPERTS * RANK
FK = T // P
EK = ER // P
HALF = T // 2
ER2 = ER // 2
DW = ER + EXPERTS
D1 = ER2 + EXPERTS
EPS = 1e-5
SCALE = HD ** -0.5
MASKED = -1e30


class Batch:

    def __init__(self, j, c):
        self.j, self.c = j, c

    def count(self, per, k):
        fixed = per * self.c + k
        return fixed if isinstance(self.j, int) and self.j == 0 else self.j * (2 * per) + fixed

    def turn(self, k):
        fixed = 16 * (self.c // 2 + k)
        return fixed if isinstance(self.j, int) and self.j == 0 else self.j * 16 + fixed

    @property
    def parity(self):
        return self.c % 2

    def row(self, eng):
        return self.c if isinstance(self.j, int) and self.j == 0 else eng.snap(self.j * 2 + self.c)


def build(nc, x, ctx, wqkvo, biases, down_w, up_w, ident_in, masks_in, consts_in, out):
    with ExitStack() as stack:
        def sb(name, shape, dt=F32):
            return stack.enter_context(nc.sbuf_tensor(name, shape, dt))

        def psum(name, cols):
            return stack.enter_context(nc.psum_tensor(name, [P, cols], F32))

        def sem(name):
            return stack.enter_context(nc.semaphore(name))

        w_split = sb("w_split", [P, 2, 4 * P], F32R)
        down_split = sb("down_split", [P, 2, FK * DW], F32R)
        up_split = sb("up_split", [P, 2, EK * T], F32R)
        ident = sb("ident", [P, P])
        mask_rows = sb("mask_rows", [P, P], BF16)
        mask_cols = sb("mask_cols", [P, CW], BF16)
        bias = sb("bias", [P, 4])
        bq_scaled = sb("bq_scaled", [P, 1])
        consts = sb("consts", [P, 4 + EXPERTS])
        q_diag = sb("q_diag", [P, 3, HEADS * QT * HT], BF16)
        v_diag = sb("v_diag", [P, PAIRS * PW * HT])
        raw = sb("raw", [P, T])
        src_split = sb("src_split", [P, 2, T], F32R)
        resid_pair = sb("resid_pair", [P, 2 * T])
        resid = [resid_pair[:, n * T:(n + 1) * T] for n in range(2)]
        q_sb = sb("q_sb", [P, T])
        q_parts = sb("q_parts", [P, 3, T], BF16)
        k_sb = sb("k_sb", [P, T])
        k_parts = sb("k_parts", [P, 3, KPAD], BF16)
        v_sb = sb("v_sb", [P, KPAD])
        v_t = sb("v_t", [P, 2, PW * HT])
        prob = sb("prob", [P, 2 * CW])
        prob_t = sb("prob_t", [P, TILES * KT])
        attn = sb("attn", [P, T])
        xn2 = sb("xn2", [P, T])
        attn_split = sb("attn_split", [P, 2, T], F32R)
        xt_split = sb("xt_split", [P, 2, T], F32R)
        h_sb = sb("h_sb", [P, ER])
        ht_split = sb("ht_split", [P, 2, ER], F32R)
        row_max = sb("row_max", [P, TILES])
        row_sum = sb("row_sum", [P, TILES])
        row_inv = sb("row_inv", [P, TILES])
        stats = sb("stats", [P, 2, 2, 6])
        moments = sb("moments", [P, 2, 2])
        var_eps = sb("var_eps", [P, 2])
        rstd = sb("rstd", [P, 2])
        shift = sb("shift", [P, 2])
        logits = sb("logits", [P, EXPERTS])
        top = sb("top", [P, 8])
        top_at = sb("top_at", [P, 8], U32)
        top_atf = sb("top_atf", [P, 2])
        gate = sb("gate", [P, 5])
        fences = sb("fences", [P, 3])
        pick = sb("pick", [P, 3, EXPERTS])

        bank_a = psum("bank_a", T)
        bank_b = [psum(f"bank_b{m}", CW) for m in range(CHUNKS)]
        bank_c = psum("bank_c", T)

        small_in = sem("small_in")
        weights_in = [sem(f"weights_in{n}") for n in range(5)]
        weights_hi, weights_lo = sem("weights_hi"), sem("weights_lo")
        masks_ready, bq_ready = sem("masks_ready"), sem("bq_ready")
        pads_zero = sem("pads_zero")
        q_diag_zero, v_diag_zero = sem("q_diag_zero"), sem("v_diag_zero")
        raw_in = sem("raw_in")
        resid_in = [sem("resid_in0"), sem("resid_in1")]
        stored = [sem("stored0"), sem("stored1")]
        q_placed, v_placed = sem("q_placed"), sem("v_placed")
        q_done, k_done, v_done = sem("q_done"), sem("k_done"), sem("v_done")
        down_done, pv_done, ht_done = sem("down_done"), sem("pv_done"), sem("ht_done")
        scores_done, o_done = sem("scores_done"), sem("o_done")
        up_done, xt_done = sem("up_done"), sem("xt_done")
        q_out, k_out, v_out = sem("q_out"), sem("k_out"), sem("v_out")
        q_part1, q_part2, k_part1, k_part2 = sem("q_part1"), sem("q_part2"), sem("k_part1"), sem("k_part2")
        gap_exp, even_out, ht_hi = sem("gap_exp"), sem("even_out"), sem("ht_hi")
        exp_done, xt_hi = sem("exp_done"), sem("xt_hi")
        v_t_done, gate_step, h_done = sem("v_t_done"), sem("gate_step"), sem("h_done")
        attn_done, attn_hi = sem("attn_done"), sem("attn_hi")
        ln1_step, xn_done, xn_hi = sem("ln1_step"), sem("xn_done"), sem("xn_hi")
        ht_lo, max_done, shifted = sem("ht_lo"), sem("max_done"), sem("shifted")
        sum_done, inv_done, prob_t_done = sem("sum_done"), sem("inv_done"), sem("prob_t_done")
        x1_done, ln2_step, xn2_done = sem("x1_done"), sem("ln2_step"), sem("xn2_done")
        ctx_hi, result_done, xt_lo = sem("ctx_hi"), sem("result_done"), sem("xt_lo")
        q_rest, q_part3, k_rest, k_part3 = sem("q_rest"), sem("q_part3"), sem("k_rest"), sem("k_part3")
        attn_lo, rstd1, xn_lo = sem("attn_lo"), sem("rstd1"), sem("xn_lo")
        prob_done, rstd2, ctx_lo = sem("prob_done"), sem("rstd2"), sem("ctx_lo")

        def piece(source, buffer, parts, lo, hi):
            return source[:, lo:hi], buffer[:, 0:hi - lo], parts[:, :, lo:hi]
        pieces = (piece(wqkvo, attn, w_split, 0, 4 * P),
                  piece(down_w, prob_t, down_split, 0, 3 * DW),
                  piece(down_w, resid_pair, down_split, 3 * DW, 6 * DW),
                  piece(up_w, v_diag, up_split, 0, EK * T),
                  piece(down_w, resid_pair, down_split, 6 * DW, FK * DW))

        block = stack.enter_context(nc.Block())

        def steps(eng, step):
            first, tail = 3, 5
            loops = (BATCHES + 2 - first - tail) // 2

            def peeled(i):
                step(*(Batch(0, i + d) if 0 <= i + d < BATCHES else None for d in (2, 1, 0, -1, -2)))

            for i in range(-2, first):
                peeled(i)
            with eng.Fori(0, loops) as j:
                for u in range(2):
                    step(*(Batch(j, first + u + d) for d in (2, 1, 0, -1, -2)))
            for i in range(first + 2 * loops, BATCHES + 2):
                peeled(i)

        @block.sync
        def _(sp):
            def load_piece(n):
                source, buffer, _ = pieces[n]
                sp.dma_start(buffer, source).then_inc(weights_in[n], 16)

            def place_q(half):
                w = QT * HT
                for h in range(HEADS):
                    rows = slice(HD * h, HD * (h + 1))
                    sp.dma_start(q_diag[rows, :, h * w:(h + 1) * w],
                                 q_parts[rows, :, half * w:(half + 1) * w]).then_inc(q_placed, 16)

            def place_v(half):
                w = PW * HT
                for g in range(PAIRS):
                    rows = slice(PW * g, PW * (g + 1))
                    sp.dma_start(v_diag[rows, g * w:(g + 1) * w],
                                 v_t[rows, half, :]).then_inc(v_placed, 16)

            def constants():
                load_piece(0)
                sp.dma_start(consts[:], consts_in).then_inc(small_in, 16)
                sp.dma_start(bias[:], biases).then_inc(small_in, 16)
                sp.dma_start(prob[:, 0:P + CW], masks_in).then_inc(small_in, 16)
                sp.dma_start(ident[:], ident_in).then_inc(small_in, 16)

            def step(later, ahead, cur, prev, old):
                later_row, ahead_row, prev_row, old_row = (b and b.row(sp) for b in (later, ahead, prev, old))
                if prev:
                    if prev.c >= 2:
                        sp.wait_ge(stored[prev.parity], prev.turn(0))
                    if prev.c <= 1:
                        sp.wait_ge(weights_lo, 5)
                    sp.dma_start(resid[prev.parity], x[prev_row]).then_inc(resid_in[prev.parity], 16)
                if cur:
                    sp.wait_ge(scores_done, cur.count(CHUNKS, 2))
                    place_q(1)
                if ahead:
                    sp.wait_ge(xn_lo, ahead.count(1, 1))
                    sp.dma_start(raw[:], ctx[ahead_row]).then_inc(raw_in, 16)
                    if ahead.c == 0:
                        load_piece(1)
                        load_piece(2)
                        load_piece(3)
                    if ahead.c == 1:
                        sp.wait_ge(weights_lo, 3)
                        load_piece(4)
                if cur:
                    if cur.c >= 1:
                        sp.wait_ge(pv_done, cur.count(CHUNKS, 0))
                    else:
                        sp.wait_ge(v_diag_zero, 1)
                    sp.wait_ge(v_t_done, cur.count(CHUNKS, 2))
                    place_v(0)
                if later:
                    if later.c >= 1:
                        sp.wait_ge(ctx_lo, later.count(1, 0))
                    sp.dma_start(raw[:], x[later_row]).then_inc(raw_in, 16)
                    if later.c == 0:
                        constants()
                if ahead:
                    if ahead.c >= 1:
                        sp.wait_ge(scores_done, ahead.count(CHUNKS, 0))
                    else:
                        sp.wait_ge(q_diag_zero, 1)
                    sp.wait_ge(q_part3, ahead.count(1, 1))
                    place_q(0)
                if cur:
                    sp.wait_ge(pv_done, cur.count(CHUNKS, 2))
                    sp.wait_ge(v_t_done, cur.count(CHUNKS, 4))
                    place_v(1)
                if old:
                    sp.wait_ge(result_done, old.count(2, 2))
                    sp.dma_start(out[old_row], resid[old.parity]).then_inc(stored[old.parity], 16)

            steps(sp, step)
            sp.wait_ge(stored[0], 16 * (BATCHES // 2))
            sp.wait_ge(stored[1], 16 * (BATCHES // 2))

        @block.tensor
        def _(pe):
            pe.wait_ge(weights_lo, 1)
            pe.wait_ge(masks_ready, 2)
            pe.wait_ge(pads_zero, 4)

            def one_pass(n, dst, st, st_cols, mv, mv_cols, start, stop):
                s, m = ((0, 0), (0, 1), (1, 0))[n]
                return nc.tensor.matmul(dst, st[:, s, st_cols], mv[:, m, mv_cols],
                                        start=start and n == 0, stop=stop and n == 2)

            def product(*operands):
                for n in range(3):
                    last = one_pass(n, *operands)
                return last

            def project_pass(n, bank, which, source):
                half = slice(n // 3 * HALF, (n // 3 + 1) * HALF)
                return one_pass(n % 3, bank[:, half], w_split, slice(which * P, (which + 1) * P),
                                source, half, True, True)

            def tiles(m, s):
                return [(t, m % 2 * CT + t) for t in range(s * CT // GROUPS, (s + 1) * CT // GROUPS)]

            def open_scores(cur, m):
                if m >= 2 or cur.c >= 1:
                    pe.wait_ge(shifted, cur.count(CHUNKS, m - 1))
                nc.tensor.matmul(bank_b[m % 2][:], mask_rows[:], mask_cols[:],
                                 start=True, stop=False, skip_group_check=True)

            def scores_group(m, s):
                for t, n in tiles(m, s):
                    at = (m * CT + t) * QT
                    for a, b in ((0, 2), (1, 1), (2, 0), (0, 1), (1, 0), (0, 0)):
                        last = nc.tensor.matmul(bank_b[m % 2][:, t * KT:(t + 1) * KT],
                                                q_diag[:, a, n:n + (P - 1) * HT + 1:HT],
                                                k_parts[:, b, at:at + KT], start=False,
                                                stop=t == CT - 1 and a == b == 0,
                                                skip_group_check=True)
                if s == GROUPS - 1:
                    last.then_inc(scores_done, 1)

            def weighted_group(m, s):
                for t, n in tiles(m, s):
                    at = (m * CT + t) * KT
                    last = nc.tensor.matmul(bank_b[2 + m % 2][:, t * PW:(t + 1) * PW],
                                            v_diag[:, n:n + (P - 1) * HT + 1:HT],
                                            prob_t[:, at:at + KT], start=True, stop=True)
                if s == GROUPS - 1:
                    last.then_inc(pv_done, 1)

            def transposes(bank, source, blocks):
                for f in blocks:
                    last = nc.tensor.transpose(bank[:, f * P:(f + 1) * P],
                                               source[:, f * P:(f + 1) * P], ident[:])
                return last

            def down(n, f):
                lo, hi = ((0, D1), (D1, DW))[n]
                last = product(bank_a[:, n * HALF:n * HALF + hi - lo], xt_split,
                               slice(f * P, (f + 1) * P), down_split,
                               slice(f * DW + lo, f * DW + hi), f == 0, f == FK - 1)
                if f == FK - 1:
                    last.then_inc(down_done, 1)

            def up(n, e):
                last = product(bank_a[:, n * HALF:(n + 1) * HALF], ht_split,
                               slice(e * P, (e + 1) * P), up_split,
                               slice(e * T + n * HALF, e * T + (n + 1) * HALF),
                               e == 0, e == EK - 1)
                if e == EK - 1:
                    last.then_inc(up_done, 1)

            def step(later, ahead, cur, prev, old):
                if cur:
                    if old:
                        pe.wait_ge(x1_done, old.count(2, 2))
                    else:
                        pe.wait_ge(k_out, cur.count(1, 1))
                    for n in range(6):
                        last = project_pass(n, bank_c, 2, src_split)
                    last.then_inc(v_done, 1)
                    pe.wait_ge(k_part3, cur.count(1, 1))
                    pe.wait_ge(q_placed, cur.count(32 * HEADS, 16 * HEADS))
                for m in range(2):
                    if m == 1 and old:
                        pe.wait_ge(xn2_done, old.count(1, 1))
                        if old.c >= 1:
                            pe.wait_ge(result_done, old.count(2, 0))
                        transposes(bank_a, xn2, range(0, 4)).then_inc(xt_done, 1)
                        transposes(bank_a, xn2, range(4, FK)).then_inc(xt_done, 1)
                    if cur:
                        open_scores(cur, m)
                        for s in range(GROUPS):
                            scores_group(m, s)
                if prev:
                    pe.wait_ge(v_placed, prev.count(32 * PAIRS, 32 * PAIRS))
                if old:
                    pe.wait_ge(xt_hi, old.count(2, 2))
                    pe.wait_ge(xt_lo, old.count(2, 2))
                    if old.c == 0:
                        pe.wait_ge(weights_lo, 5)
                for m in range(2, CHUNKS):
                    if prev:
                        pe.wait_ge(prob_t_done, prev.count(CHUNKS, m + 1))
                        pe.wait_ge(attn_done, prev.count(CHUNKS, m - 1))
                    for s in range(GROUPS):
                        if prev:
                            weighted_group(m, s)
                        if old:
                            down(0, (m - 2) * GROUPS + s)
                        if m == 2 and ahead:
                            if s == 0:
                                pe.wait_ge(xn_hi, ahead.count(1, 1))
                                pe.wait_ge(xn_lo, ahead.count(1, 1))
                                if cur:
                                    pe.wait_ge(v_out, cur.count(1, 1))
                            for n in ((0, 1), (2,), (3, 4), (5,))[s]:
                                last = project_pass(n, bank_c, 0, src_split)
                            if s == GROUPS - 1:
                                last.then_inc(q_done, 1)
                if cur:
                    pe.wait_ge(q_placed, cur.count(32 * HEADS, 32 * HEADS))
                for m in range(2, CHUNKS):
                    if cur:
                        open_scores(cur, m)
                    for s in range(GROUPS):
                        if cur:
                            scores_group(m, s)
                        if m == 2 and old:
                            down(1, 2 * s)
                            down(1, 2 * s + 1)
                        if m == 3 and ahead:
                            if s == 0:
                                pe.wait_ge(ctx_hi, ahead.count(1, 1))
                                pe.wait_ge(ctx_lo, ahead.count(1, 1))
                                pe.wait_ge(q_out, ahead.count(1, 1))
                            for n in ((0, 1), (2,), (3, 4), (5,))[s]:
                                last = project_pass(n, bank_c, 1, src_split)
                            if s == GROUPS - 1:
                                last.then_inc(k_done, 1)
                        if m == 3 and s == 2 and old:
                            pe.wait_ge(h_done, old.count(2, 2))
                            transposes(bank_a, h_sb, range(EK)).then_inc(ht_done, 1)
                if cur:
                    pe.wait_ge(v_placed, cur.count(32 * PAIRS, 16 * PAIRS))
                for m in range(2):
                    if cur:
                        pe.wait_ge(prob_t_done, cur.count(CHUNKS, m + 1))
                        if cur.c >= 1:
                            pe.wait_ge(attn_done, cur.count(CHUNKS, m - 1))
                    for s in range(GROUPS):
                        if cur:
                            weighted_group(m, s)
                        if m == 0 and prev:
                            if s == 0:
                                pe.wait_ge(attn_hi, prev.count(1, 1))
                                pe.wait_ge(attn_lo, prev.count(1, 1))
                                if ahead:
                                    pe.wait_ge(k_out, ahead.count(1, 1))
                                elif cur:
                                    pe.wait_ge(v_out, cur.count(1, 1))
                            for n in ((0, 1), (2,), (3, 4), (5,))[s]:
                                last = project_pass(n, bank_c, 3, attn_split)
                                if n % 3 == 2:
                                    last.then_inc(o_done, 1)
                        if old:
                            if m == s == 0:
                                pe.wait_ge(ht_hi, old.count(1, 1))
                                pe.wait_ge(ht_lo, old.count(1, 1))
                            up(m, s)

            steps(pe, step)

        @block.scalar
        def _(act):
            def split_hi(n):
                _, exact, parts = pieces[n]
                act.wait_ge(weights_in[n], 16)
                nc.scalar.activation(parts[:, 0, :], exact, ACT.Copy).then_inc(weights_hi, 1)

            split_hi(0)
            act.wait_ge(small_in, 16 * 4)
            nc.scalar.activation(mask_rows[:], prob[:, 0:P], ACT.Copy).then_inc(masks_ready, 1)
            nc.scalar.activation(mask_cols[:], prob[:, P:P + CW], ACT.Copy).then_inc(masks_ready, 1)
            nc.scalar.activation(bq_scaled[:], bias[:, 0:1], ACT.Copy, scale=SCALE).then_inc(bq_ready, 1)

            def even_heads(b, m):
                act.wait_ge(pv_done, b.count(CHUNKS, m + 1))
                if m == 0 and b.c >= 1:
                    act.wait_ge(attn_lo, b.count(1, 0))
                src = bank_b[2 + m % 2][:].rearrange("p (n h i) -> p n h i", h=2, i=QT)
                dst = attn[:, m * CT * QT:(m + 1) * CT * QT]
                nc.scalar.activation(dst.rearrange("p (n i) -> p n i", i=QT), src[:, :, 0, :],
                                     ACT.Copy, scale=consts[:, 0:1]).then_inc(even_out, 1)

            def exponentials(cur, m):
                act.wait_ge(shifted, cur.count(CHUNKS, m + 1))
                half = slice(m % 2 * CW, (m % 2 + 1) * CW)
                nc.scalar.activation(prob[:, half], prob[:, half], ACT.Exp).then_inc(exp_done, 1)

            def step(later, ahead, cur, prev, old):
                if old:
                    for n in range(2):
                        act.wait_ge(xt_done, old.count(2, n + 1))
                        if n == 0 and old.c >= 1:
                            act.wait_ge(down_done, old.count(2, 0))
                        half = slice(n * HALF, (n + 1) * HALF)
                        nc.scalar.activation(xt_split[:, 0, half], bank_a[:, half],
                                             ACT.Copy).then_inc(xt_hi, 1)
                if cur:
                    act.wait_ge(v_done, cur.count(1, 1))
                    if cur.c >= 1:
                        act.wait_ge(v_t_done, cur.count(CHUNKS, 0))
                    nc.scalar.activation(v_sb[:, PAD_LEFT:PAD_LEFT + T], bank_c[:], ACT.Identity,
                                         bias=bias[:, 2:3]).then_inc(v_out, 1)
                    if cur.c == 0:
                        split_hi(1)
                        split_hi(2)
                        split_hi(3)
                    exponentials(cur, 0)
                    exponentials(cur, 1)
                if ahead:
                    act.wait_ge(q_done, ahead.count(1, 1))
                    if ahead.c >= 1:
                        act.wait_ge(q_part3, ahead.count(1, 0))
                    else:
                        act.wait_ge(bq_ready, 1)
                    nc.scalar.activation(q_sb[:].rearrange("p (h i n) -> p h n i", h=2, n=HT),
                                         bank_c[:].rearrange("p (h n i) -> p h n i", h=2, i=QT),
                                         ACT.Identity, bias=bq_scaled[:], scale=SCALE).then_inc(q_out, 1)
                    act.wait_ge(q_out, ahead.count(1, 1))
                    if ahead.c >= 1:
                        act.wait_ge(q_placed, ahead.count(32 * HEADS, 0))
                    nc.scalar.activation(q_parts[:, 0, :], q_sb[:], ACT.Copy).then_inc(q_part1, 1)
                if prev:
                    even_heads(prev, 2)
                if prev:
                    even_heads(prev, 3)
                if old:
                    act.wait_ge(gate_step, old.count(13, 7))
                    nc.scalar.activation(gate[:, 1:2], gate[:, 0:1], ACT.Exp).then_inc(gap_exp, 1)
                if ahead:
                    act.wait_ge(q_rest, ahead.count(1, 1))
                    nc.scalar.activation(q_parts[:, 1, :], q_sb[:], ACT.Copy).then_inc(q_part2, 1)
                if cur:
                    exponentials(cur, 2)
                if old:
                    act.wait_ge(ht_done, old.count(1, 1))
                    if old.c >= 1:
                        act.wait_ge(up_done, old.count(2, 0))
                    nc.scalar.activation(ht_split[:, 0, :], bank_a[:, 0:ER], ACT.Copy).then_inc(ht_hi, 1)
                if ahead:
                    act.wait_ge(k_done, ahead.count(1, 1))
                    if ahead.c >= 1:
                        act.wait_ge(k_part3, ahead.count(1, 0))
                    nc.scalar.activation(k_sb[:], bank_c[:], ACT.Identity,
                                         bias=bias[:, 1:2]).then_inc(k_out, 1)
                    act.wait_ge(k_out, ahead.count(1, 1))
                    if ahead.c >= 1:
                        act.wait_ge(scores_done, ahead.count(CHUNKS, 0))
                    nc.scalar.activation(k_parts[:, 0, PAD_LEFT:PAD_LEFT + T], k_sb[:],
                                         ACT.Copy).then_inc(k_part1, 1)
                if cur:
                    exponentials(cur, 3)
                if ahead:
                    act.wait_ge(k_rest, ahead.count(1, 1))
                    nc.scalar.activation(k_parts[:, 1, PAD_LEFT:PAD_LEFT + T], k_sb[:],
                                         ACT.Copy).then_inc(k_part2, 1)
                if cur:
                    even_heads(cur, 0)
                if prev:
                    act.wait_ge(ln2_step, prev.count(6, 6))
                    if prev.c >= 1:
                        act.wait_ge(xt_done, prev.count(2, 0))
                    nc.scalar.activation(xn2[:], resid[prev.parity], ACT.Identity, bias=shift[:, 1:2],
                                         scale=rstd[:, 1:2]).then_inc(xn2_done, 1)
                if later:
                    act.wait_ge(ln1_step, later.count(6, 6))
                    nc.scalar.activation(raw[:], raw[:], ACT.Identity, bias=shift[:, 0:1],
                                         scale=rstd[:, 0:1]).then_inc(xn_done, 1)
                if cur:
                    even_heads(cur, 1)
                    if cur.c == 0:
                        split_hi(4)

            steps(act, step)

        @block.vector
        def _(dve):
            def split_lo(n):
                _, exact, parts = pieces[n]
                dve.wait_ge(weights_hi, n + 1)
                nc.vector.tensor_tensor(parts[:, 1, :], exact, parts[:, 0, :].bitcast(F32),
                                        ALU.subtract).then_inc(weights_lo, 1)

            split_lo(0)
            dve.wait_ge(small_in, 16 * 4)

            def fence(semaphore, which):
                nc.vector.memset(fences[:, which:which + 1], 0.0).then_inc(semaphore, 1)

            def layernorm_stats(which, source, semaphore, batch):
                for n in range(2):
                    nc.vector.bn_stats(stats[:, which, n, :],
                                       source[:, n * HALF:(n + 1) * HALF]).then_inc(semaphore, 1)
                dve.wait_ge(semaphore, batch.count(6, 2))
                fence(semaphore, which)
                nc.vector.bn_aggr(moments[:, which, :],
                                  stats[:, which, :, :].rearrange("p a b -> p (a b)")).then_inc(semaphore, 1)
                dve.wait_ge(semaphore, batch.count(6, 4))
                nc.vector.tensor_scalar(var_eps[:, which:which + 1], moments[:, which, 1:2], EPS, None,
                                        ALU.add).then_inc(semaphore, 1)

            def layernorm_shift(which, semaphore, batch):
                nc.vector.scalar_tensor_tensor(shift[:, which:which + 1], moments[:, which, 0:1], -1.0,
                                               rstd[:, which:which + 1], ALU.mult,
                                               ALU.mult).then_inc(semaphore, 1)

            def join_heads(prev, m):
                dve.wait_ge(even_out, prev.count(CHUNKS, m + 1))
                src = bank_b[2 + m % 2][:].rearrange("p (n h i) -> p n h i", h=2, i=QT)
                dst = attn[:, m * CT * QT:(m + 1) * CT * QT].rearrange("p (n i) -> p n i", i=QT)
                nc.vector.scalar_tensor_tensor(dst, src[:, :, 1, :], consts[:, 1:2], dst,
                                               ALU.mult, ALU.add).then_inc(attn_done, 1)

            def choose_experts(old):
                dve.wait_ge(down_done, old.count(2, 1))
                nc.vector.tensor_copy(logits[:], bank_a[:, ER2:D1]).then_inc(gate_step, 1)
                dve.wait_ge(gate_step, old.count(13, 1))
                fence(gate_step, 2)
                nc.vector.max(top[:], logits[:]).then_inc(gate_step, 1)
                dve.wait_ge(gate_step, old.count(13, 3))
                fence(gate_step, 2)
                nc.vector.max_index(top_at[:], top[:], logits[:]).then_inc(gate_step, 1)
                dve.wait_ge(gate_step, old.count(13, 5))
                nc.vector.tensor_copy(top_atf[:], top_at[:, 0:2]).then_inc(gate_step, 1)
                nc.vector.tensor_tensor(gate[:, 0:1], top[:, 1:2], top[:, 0:1],
                                        ALU.subtract).then_inc(gate_step, 1)
                dve.wait_ge(gap_exp, old.count(1, 1))
                nc.vector.tensor_scalar(gate[:, 2:3], gate[:, 1:2], 1.0, None, ALU.add).then_inc(gate_step, 1)
                dve.wait_ge(gate_step, old.count(13, 8))
                nc.vector.reciprocal(gate[:, 3:4], gate[:, 2:3]).then_inc(gate_step, 1)
                dve.wait_ge(gate_step, old.count(13, 9))
                nc.vector.tensor_tensor(gate[:, 4:5], gate[:, 1:2], gate[:, 3:4], ALU.mult).then_inc(gate_step, 1)
                dve.wait_ge(gate_step, old.count(13, 10))
                for n in range(2):
                    nc.vector.tensor_scalar(pick[:, n, :], consts[:, 4:4 + EXPERTS],
                                            top_atf[:, n:n + 1], gate[:, 3 + n:4 + n],
                                            ALU.is_equal, ALU.mult).then_inc(gate_step, 1)
                dve.wait_ge(gate_step, old.count(13, 12))
                nc.vector.tensor_tensor(pick[:, 2, :], pick[:, 0, :], pick[:, 1, :],
                                        ALU.add).then_inc(gate_step, 1)
                dve.wait_ge(gate_step, old.count(13, 13))

            def weigh_experts(old, n):
                experts = slice(n * EXPERTS // 2, (n + 1) * EXPERTS // 2)
                dve.wait_ge(down_done, old.count(2, n + 1))
                if n == 0 and old.c >= 1:
                    dve.wait_ge(ht_done, old.count(1, 0))
                nc.vector.tensor_tensor(
                    h_sb[:, n * ER2:(n + 1) * ER2].rearrange("p (e r) -> p e r", r=RANK),
                    bank_a[:, n * HALF:n * HALF + ER2].rearrange("p (e r) -> p e r", r=RANK),
                    pick[:, 2, experts].unsqueeze(2).broadcast_to([P, EXPERTS // 2, RANK]),
                    ALU.mult).then_inc(h_done, 1)

            def scores_shift(cur, m):
                cols = slice(m * CT, (m + 1) * CT)
                scores = bank_b[m % 2][:].rearrange("p (n j) -> p n j", j=KT)
                dve.wait_ge(scores_done, cur.count(CHUNKS, m + 1))
                nc.vector.tensor_reduce(row_max[:, cols], scores, AX_X, ALU.max).then_inc(max_done, 1)
                dve.wait_ge(max_done, cur.count(CHUNKS, m + 1))
                if m >= 2 or cur.c >= 1:
                    dve.wait_ge(prob_t_done, cur.count(CHUNKS, m - 1))
                nc.vector.tensor_tensor(prob[:, m % 2 * CW:(m % 2 + 1) * CW].rearrange("p (n j) -> p n j", j=KT), scores,
                                        row_max[:, cols].unsqueeze(2).broadcast_to([P, CT, KT]),
                                        ALU.subtract).then_inc(shifted, 1)

            def weights_sum(cur, m):
                cols = slice(m * CT, (m + 1) * CT)
                dve.wait_ge(exp_done, cur.count(CHUNKS, m + 1))
                nc.vector.tensor_reduce(row_sum[:, cols],
                                        prob[:, m % 2 * CW:(m % 2 + 1) * CW].rearrange("p (n j) -> p n j", j=KT),
                                        AX_X, ALU.add).then_inc(sum_done, 1)
                dve.wait_ge(sum_done, cur.count(CHUNKS, m + 1))
                if m == 0 and cur.c >= 1:
                    dve.wait_ge(prob_done, cur.count(CHUNKS, 0))
                nc.vector.reciprocal(row_inv[:, cols], row_sum[:, cols]).then_inc(inv_done, 1)

            def weights_transpose(cur, m):
                dve.wait_ge(prob_done, cur.count(CHUNKS, m + 1))
                if cur.c >= 1:
                    dve.wait_ge(pv_done, cur.count(CHUNKS, m - 3))
                nc.vector.transpose(prob_t[:, m * CW:(m + 1) * CW],
                                    prob[:, m % 2 * CW:(m % 2 + 1) * CW]).then_inc(prob_t_done, 1)

            def add_mixture(old, n):
                y = resid[old.parity][:, n * HALF:(n + 1) * HALF]
                dve.wait_ge(up_done, old.count(2, n + 1))
                nc.vector.tensor_tensor(y, bank_a[:, n * HALF:(n + 1) * HALF], y,
                                        ALU.add).then_inc(result_done, 1)

            def step(later, ahead, cur, prev, old):
                if ahead:
                    dve.wait_ge(xn_done, ahead.count(1, 1))
                    if cur:
                        dve.wait_ge(v_done, cur.count(1, 1))
                    nc.vector.tensor_copy(src_split[:, 0, :], raw[:]).then_inc(xn_hi, 1)
                if old:
                    for n in range(2):
                        half = slice(n * HALF, (n + 1) * HALF)
                        dve.wait_ge(xt_hi, old.count(2, n + 1))
                        nc.vector.tensor_tensor(xt_split[:, 1, half], bank_a[:, half],
                                                xt_split[:, 0, half].bitcast(F32),
                                                ALU.subtract).then_inc(xt_lo, 1)
                if cur:
                    scores_shift(cur, 0)
                if cur:
                    if cur.c == 0:
                        split_lo(1)
                        split_lo(2)
                        split_lo(3)
                    weights_sum(cur, 0)
                    scores_shift(cur, 1)
                if prev:
                    join_heads(prev, 2)
                if cur:
                    weights_transpose(cur, 0)
                    weights_sum(cur, 1)
                    for h in range(2):
                        dve.wait_ge(v_out, cur.count(1, 1))
                        if cur.c >= 1:
                            dve.wait_ge(v_placed, cur.count(32 * PAIRS, 16 * PAIRS * (h - 1)))
                        windows = bass.AP(tensor=v_sb[:].tensor, offset=h * HT * QT,
                                          ap=[[KPAD, P], [QT, HT], [1, KT]])
                        nc.vector.transpose(v_t[:, h, :].rearrange("p (c n) -> p n c", n=HT),
                                            windows).then_inc(v_t_done, 2)
                if ahead:
                    dve.wait_ge(raw_in, ahead.count(32, 32))
                    dve.wait_ge(q_done, ahead.count(1, 1))
                    nc.vector.tensor_copy(src_split[:, 0, :], raw[:]).then_inc(ctx_hi, 1)
                if prev:
                    join_heads(prev, 3)
                    dve.wait_ge(attn_done, prev.count(CHUNKS, CHUNKS))
                    if prev.c >= 1:
                        dve.wait_ge(o_done, prev.count(2, 0))
                    nc.vector.tensor_copy(attn_split[:, 0, :], attn[:]).then_inc(attn_hi, 1)
                if old:
                    choose_experts(old)
                    weigh_experts(old, 0)
                if cur:
                    weights_transpose(cur, 1)
                if old:
                    weigh_experts(old, 1)
                if cur:
                    scores_shift(cur, 2)
                    weights_sum(cur, 2)
                if old:
                    dve.wait_ge(ht_hi, old.count(1, 1))
                    nc.vector.tensor_tensor(ht_split[:, 1, :], bank_a[:, 0:ER],
                                            ht_split[:, 0, :].bitcast(F32),
                                            ALU.subtract).then_inc(ht_lo, 1)
                if cur:
                    scores_shift(cur, 3)
                if prev:
                    x1 = resid[prev.parity]
                    dve.wait_ge(resid_in[prev.parity], prev.turn(1))
                    for n in range(2):
                        half = slice(n * HALF, (n + 1) * HALF)
                        dve.wait_ge(o_done, prev.count(2, n + 1))
                        nc.vector.scalar_tensor_tensor(x1[:, half], bank_c[:, half], bias[:, 3:4],
                                                       x1[:, half], ALU.add,
                                                       ALU.add).then_inc(x1_done, 1)
                    dve.wait_ge(x1_done, prev.count(2, 2))
                    layernorm_stats(1, x1, ln2_step, prev)
                if later:
                    dve.wait_ge(raw_in, later.count(32, 16))
                    layernorm_stats(0, raw, ln1_step, later)
                if cur:
                    weights_transpose(cur, 2)
                    weights_sum(cur, 3)
                if cur:
                    join_heads(cur, 0)
                if prev:
                    dve.wait_ge(rstd2, prev.count(1, 1))
                    layernorm_shift(1, ln2_step, prev)
                if later:
                    dve.wait_ge(rstd1, later.count(1, 1))
                    layernorm_shift(0, ln1_step, later)
                if old:
                    add_mixture(old, 0)
                if cur:
                    weights_transpose(cur, 3)
                    join_heads(cur, 1)
                if old:
                    add_mixture(old, 1)
                if cur and cur.c == 0:
                    split_lo(4)

            steps(dve, step)

        @block.gpsimd
        def _(pool):
            for padded in (k_parts[:], v_sb[:].unsqueeze(1)):
                nc.gpsimd.memset(padded[:, :, 0:PAD_LEFT], 0.0).then_inc(pads_zero, 1)
                nc.gpsimd.memset(padded[:, :, PAD_LEFT + T:KPAD], 0.0).then_inc(pads_zero, 1)
            nc.gpsimd.memset(q_diag[:], 0.0).then_inc(q_diag_zero, 1)
            pool.wait_ge(small_in, 16 * 4)

            def weights_norm(cur, m):
                cols = slice(m * CT, (m + 1) * CT)
                pool.wait_ge(inv_done, cur.count(CHUNKS, m + 1))
                p3 = prob[:, m % 2 * CW:(m % 2 + 1) * CW].rearrange("p (n j) -> p n j", j=KT)
                nc.gpsimd.tensor_tensor(p3, p3, row_inv[:, cols].unsqueeze(2).broadcast_to([P, CT, KT]),
                                        ALU.mult).then_inc(prob_done, 1)

            def step(later, ahead, cur, prev, old):
                if ahead:
                    pool.wait_ge(xn_hi, ahead.count(1, 1))
                    nc.gpsimd.tensor_tensor(src_split[:, 1, :], raw[:], src_split[:, 0, :].bitcast(F32),
                                            ALU.subtract).then_inc(xn_lo, 1)
                if cur:
                    if cur.c == 0:
                        pool.wait_ge(weights_lo, 4)
                        nc.gpsimd.memset(v_diag[:], 0.0).then_inc(v_diag_zero, 1)
                    weights_norm(cur, 0)
                    weights_norm(cur, 1)
                if ahead:
                    pool.wait_ge(q_part1, ahead.count(1, 1))
                    nc.gpsimd.tensor_tensor(q_sb[:], q_sb[:], q_parts[:, 0, :],
                                            ALU.subtract).then_inc(q_rest, 1)
                    pool.wait_ge(ctx_hi, ahead.count(1, 1))
                    nc.gpsimd.tensor_tensor(src_split[:, 1, :], raw[:], src_split[:, 0, :].bitcast(F32),
                                            ALU.subtract).then_inc(ctx_lo, 1)
                if prev:
                    pool.wait_ge(attn_hi, prev.count(1, 1))
                    nc.gpsimd.tensor_tensor(attn_split[:, 1, :], attn[:], attn_split[:, 0, :].bitcast(F32),
                                            ALU.subtract).then_inc(attn_lo, 1)
                if ahead:
                    pool.wait_ge(q_part2, ahead.count(1, 1))
                    nc.gpsimd.tensor_tensor(q_parts[:, 2, :], q_sb[:], q_parts[:, 1, :],
                                            ALU.subtract).then_inc(q_part3, 1)
                if cur:
                    weights_norm(cur, 2)
                if ahead:
                    pool.wait_ge(k_part1, ahead.count(1, 1))
                    nc.gpsimd.tensor_tensor(k_sb[:], k_sb[:],
                                            k_parts[:, 0, PAD_LEFT:PAD_LEFT + T],
                                            ALU.subtract).then_inc(k_rest, 1)
                if ahead:
                    k_part = k_parts[:, :, PAD_LEFT:PAD_LEFT + T]
                    pool.wait_ge(k_part2, ahead.count(1, 1))
                    nc.gpsimd.tensor_tensor(k_part[:, 2, :], k_sb[:], k_part[:, 1, :],
                                            ALU.subtract).then_inc(k_part3, 1)
                if prev:
                    pool.wait_ge(ln2_step, prev.count(6, 5))
                    nc.gpsimd.tensor_tensor(rstd[:, 1:2], var_eps[:, 1:2], consts[:, 2:3],
                                            ALU.pow).then_inc(rstd2, 1)
                if later:
                    pool.wait_ge(ln1_step, later.count(6, 5))
                    nc.gpsimd.tensor_tensor(rstd[:, 0:1], var_eps[:, 0:1], consts[:, 2:3],
                                            ALU.pow).then_inc(rstd1, 1)
                if cur:
                    weights_norm(cur, 3)

            steps(pool, step)


def shape_constants():
    rows = np.arange(P)
    mask_rows = (rows[:, None] == rows[None, :] % QT).astype(np.float32)
    key = np.arange(CW) % KT
    inside = (key[None, :] >= rows[:, None]) & (key[None, :] < rows[:, None] + WINDOW)
    mask_cols = np.where(inside | (rows[:, None] >= QT), 0.0, MASKED).astype(np.float32)
    consts = np.zeros((P, 4 + EXPERTS), np.float32)
    consts[:, 0] = rows // HD % 2 == 0
    consts[:, 1] = rows // HD % 2 == 1
    consts[:, 2] = -0.5
    consts[:, 3] = EPS
    consts[:, 4:] = np.arange(EXPERTS)
    return np.eye(P, dtype=np.float32), np.concatenate([mask_rows, mask_cols], axis=1), consts


def kernel(**inputs):
    import numpy as np
    import concourse.bacc as bacc
    from concourse import mybir
    from concourse.bass_utils import run_bass_kernel_spmd

    a = {k: np.asarray(v) for k, v in inputs.items()}
    x, ctx = a["x"], a["ctx_4096"]
    wqkvo = np.concatenate([a[f"L0_xattn_W{n}"].T for n in "qkvo"], axis=1)
    biases = np.stack([a[f"L0_xattn_b{n}"] for n in "qkvo"], axis=1)
    down = a["L0_ffn_lora_A"].reshape(ER, T)
    down = np.concatenate([down[:ER2], a["L0_ffn_gate_w"], down[ER2:]], axis=0)
    down = down.T.reshape(FK, P, DW).transpose(1, 0, 2).reshape(P, FK * DW)
    up = a["L0_ffn_lora_B"].transpose(0, 2, 1).reshape(EK, P, T).transpose(1, 0, 2).reshape(P, EK * T)
    ident, masks, consts = shape_constants()

    arrays = {
        "x": x, "ctx": ctx, "wqkvo": wqkvo, "biases": biases, "down_w": down, "up_w": up,
        "ident_in": ident, "masks_in": masks, "consts_in": consts,
    }
    arrays = {k: np.ascontiguousarray(v) for k, v in arrays.items()}
    nc = bacc.Bacc("TRN2", target_bir_lowering=False, num_devices=1)
    args = [nc.dram_tensor(k, v.shape, mybir.dt.from_np(v.dtype), kind="ExternalInput").ap()
            for k, v in arrays.items()]
    out = nc.dram_tensor("out", x.shape, mybir.dt.float32, kind="ExternalOutput").ap()
    build(nc, *args, out)
    r = run_bass_kernel_spmd(nc, [arrays], core_ids=[0])
    return r.results[0]["out"]
```

```python
from contextlib import ExitStack

import numpy as np

import concourse.bass as bass
from concourse import mybir

F32 = mybir.dt.float32
F32R = mybir.dt.float32r
BF16 = mybir.dt.bfloat16
U32 = mybir.dt.uint32
ALU = mybir.AluOpType
ACT = mybir.ActivationFunctionType
AX_X = mybir.AxisListType.X

P = 128
T = 1024
BATCHES = 32
HEADS = 8
HD = P // HEADS
WINDOW = 16
PAD_LEFT = WINDOW // 2
QT = 16
KT = 32
TILES = T // QT
CHUNKS = 4
CT = TILES // CHUNKS
CW = CT * KT
HT = TILES // 2
GROUPS = 4
KPAD = T + 2 * PAD_LEFT
PAIRS = 4
PW = P // PAIRS
EXPERTS = 8
RANK = 64
ER = EXPERTS * RANK
FK = T // P
EK = ER // P
HALF = T // 2
ER2 = ER // 2
DW = ER + EXPERTS
D1 = ER2 + EXPERTS
EPS = 1e-5
SCALE = HD ** -0.5
MASKED = -1e30


class Batch:

    def __init__(self, j, c):
        self.j, self.c = j, c

    def count(self, per, k):
        fixed = per * self.c + k
        return fixed if isinstance(self.j, int) and self.j == 0 else self.j * (2 * per) + fixed

    def turn(self, k):
        fixed = 16 * (self.c // 2 + k)
        return fixed if isinstance(self.j, int) and self.j == 0 else self.j * 16 + fixed

    @property
    def parity(self):
        return self.c % 2

    def row(self, eng):
        return self.c if isinstance(self.j, int) and self.j == 0 else eng.snap(self.j * 2 + self.c)


def build(nc, x, ctx, wqkvo, biases, down_w, up_w, ident_in, masks_in, consts_in, out):
    with ExitStack() as stack:
        def sb(name, shape, dt=F32):
            return stack.enter_context(nc.sbuf_tensor(name, shape, dt))

        def psum(name, cols):
            return stack.enter_context(nc.psum_tensor(name, [P, cols], F32))

        def sem(name):
            return stack.enter_context(nc.semaphore(name))

        w_split = sb("w_split", [P, 2, 4 * P], F32R)
        down_split = sb("down_split", [P, 2, FK * DW], F32R)
        up_split = sb("up_split", [P, 2, EK * T], F32R)
        ident = sb("ident", [P, P])
        mask_rows = sb("mask_rows", [P, P], BF16)
        mask_cols = sb("mask_cols", [P, CW], BF16)
        bias = sb("bias", [P, 4])
        bq_scaled = sb("bq_scaled", [P, 1])
        consts = sb("consts", [P, 4 + EXPERTS])
        q_diag = sb("q_diag", [P, 3, HEADS * QT * HT], BF16)
        v_diag = sb("v_diag", [P, 3, PAIRS * PW * HT], BF16)
        raw = sb("raw", [P, T])
        src_split = sb("src_split", [P, 2, T], F32R)
        resid_pair = sb("resid_pair", [P, 2 * T])
        resid = [resid_pair[:, n * T:(n + 1) * T] for n in range(2)]
        q_xn2 = sb("q_xn2", [P, T])
        q_parts = sb("q_parts", [P, 3, T], BF16)
        k_parts = sb("k_parts", [P, 3, KPAD], BF16)
        kv_sb = sb("kv_sb", [P, KPAD])
        v_t = sb("v_t", [P, PW * HT])
        v_parts = sb("v_parts", [P, 3, PW * HT], BF16)
        prob = sb("prob", [P, 2 * CW])
        prob_t = sb("prob_t", [P, 2 * CW])
        prob_parts = sb("prob_parts", [P, 3, TILES * KT], BF16)
        attn = sb("attn", [P, T])
        mid_split = sb("mid_split", [P, 2, T], F32R)
        h_sb = sb("h_sb", [P, ER])
        ht_split = sb("ht_split", [P, 2, ER], F32R)
        row_max = sb("row_max", [P, TILES])
        row_sum = sb("row_sum", [P, TILES])
        row_inv = sb("row_inv", [P, TILES])
        stats = sb("stats", [P, 2, 2, 6])
        moments = sb("moments", [P, 2, 2])
        var_eps = sb("var_eps", [P, 2])
        rstd = sb("rstd", [P, 2])
        shift = sb("shift", [P, 2])
        logits = sb("logits", [P, EXPERTS])
        top = sb("top", [P, 8])
        top_at = sb("top_at", [P, 8], U32)
        top_atf = sb("top_atf", [P, 2])
        gate = sb("gate", [P, 5])
        fences = sb("fences", [P, 3])
        pick = sb("pick", [P, 3, EXPERTS])

        bank_a = psum("bank_a", T)
        bank_b = [psum(f"bank_b{m}", CW) for m in range(CHUNKS)]
        bank_c = psum("bank_c", T)

        small_in = sem("small_in")
        weights_in = [sem(f"weights_in{n}") for n in range(5)]
        weights_hi, weights_lo = sem("weights_hi"), sem("weights_lo")
        masks_ready, bq_ready = sem("masks_ready"), sem("bq_ready")
        pads_zero = sem("pads_zero")
        q_diag_zero, v_diag_zero = sem("q_diag_zero"), sem("v_diag_zero")
        raw_in = sem("raw_in")
        resid_in = [sem("resid_in0"), sem("resid_in1")]
        stored = [sem("stored0"), sem("stored1")]
        q_placed, v_placed = sem("q_placed"), sem("v_placed")
        q_done, k_done, v_done = sem("q_done"), sem("k_done"), sem("v_done")
        down_done, pv_done, ht_done = sem("down_done"), sem("pv_done"), sem("ht_done")
        scores_done, o_done = sem("scores_done"), sem("o_done")
        up_done, xt_done = sem("up_done"), sem("xt_done")
        q_out, k_out, v_out = sem("q_out"), sem("k_out"), sem("v_out")
        q_part1, q_part2, k_part1, k_part2 = sem("q_part1"), sem("q_part2"), sem("k_part1"), sem("k_part2")
        v_part1, v_part2, prob_part1, prob_part2 = sem("v_part1"), sem("v_part2"), sem("prob_part1"), sem("prob_part2")
        gap_exp, even_out, ht_hi = sem("gap_exp"), sem("even_out"), sem("ht_hi")
        exp_done, xt_hi = sem("exp_done"), sem("xt_hi")
        v_t_done, gate_step, h_done = sem("v_t_done"), sem("gate_step"), sem("h_done")
        attn_done, attn_hi = sem("attn_done"), sem("attn_hi")
        ln1_step, xn_done, xn_hi = sem("ln1_step"), sem("xn_done"), sem("xn_hi")
        ht_lo, max_done, shifted = sem("ht_lo"), sem("max_done"), sem("shifted")
        sum_done, inv_done, prob_t_done = sem("sum_done"), sem("inv_done"), sem("prob_t_done")
        x1_done, ln2_step, xn2_done = sem("x1_done"), sem("ln2_step"), sem("xn2_done")
        ctx_hi, result_done, xt_lo = sem("ctx_hi"), sem("result_done"), sem("xt_lo")
        prob_rest, prob_part3 = sem("prob_rest"), sem("prob_part3")
        v_rest, v_part3 = sem("v_rest"), sem("v_part3")
        q_rest, q_part3, k_rest, k_part3 = sem("q_rest"), sem("q_part3"), sem("k_rest"), sem("k_part3")
        attn_lo, rstd1, xn_lo = sem("attn_lo"), sem("rstd1"), sem("xn_lo")
        prob_done, rstd2, ctx_lo = sem("prob_done"), sem("rstd2"), sem("ctx_lo")

        def piece(source, buffer, at, parts, lo, hi):
            return source[:, lo:hi], buffer[:, at:at + hi - lo], parts[:, :, lo:hi]

        v_diag_f32 = v_diag[:].rearrange("p a n -> p (a n)").bitcast(F32)
        prob_parts_f32 = prob_parts[:].rearrange("p a n -> p (a n)").bitcast(F32)
        pieces = (piece(wqkvo, attn, 0, w_split, 0, 4 * P),
                  piece(down_w, v_diag_f32, EK * T, down_split, 0, 3 * DW),
                  piece(up_w, v_diag_f32, 0, up_split, 0, EK * T),
                  piece(down_w, prob_parts_f32, 0, down_split, 3 * DW, 5 * DW),
                  piece(down_w, resid_pair, 0, down_split, 5 * DW, FK * DW))

        block = stack.enter_context(nc.Block())

        def steps(eng, step):
            first, tail = 3, 5
            loops = (BATCHES + 2 - first - tail) // 2

            def peeled(i):
                step(*(Batch(0, i + d) if 0 <= i + d < BATCHES else None for d in (2, 1, 0, -1, -2)))

            for i in range(-2, first):
                peeled(i)
            with eng.Fori(0, loops) as j:
                for u in range(2):
                    step(*(Batch(j, first + u + d) for d in (2, 1, 0, -1, -2)))
            for i in range(first + 2 * loops, BATCHES + 2):
                peeled(i)

        @block.sync
        def _(sp):
            def load_piece(n):
                source, buffer, _ = pieces[n]
                sp.dma_start(buffer, source).then_inc(weights_in[n], 16)

            def place_q(half):
                w = QT * HT
                for h in range(HEADS):
                    rows = slice(HD * h, HD * (h + 1))
                    sp.dma_start(q_diag[rows, :, h * w:(h + 1) * w],
                                 q_parts[rows, :, half * w:(half + 1) * w]).then_inc(q_placed, 16)

            def place_v():
                w = PW * HT
                for g in range(PAIRS):
                    rows = slice(PW * g, PW * (g + 1))
                    sp.dma_start(v_diag[rows, :, g * w:(g + 1) * w],
                                 v_parts[rows, :, :]).then_inc(v_placed, 16)

            def constants():
                load_piece(0)
                sp.dma_start(consts[:], consts_in).then_inc(small_in, 16)
                sp.dma_start(bias[:], biases).then_inc(small_in, 16)
                sp.dma_start(prob[:, 0:P + CW], masks_in).then_inc(small_in, 16)
                sp.dma_start(ident[:], ident_in).then_inc(small_in, 16)

            def step(later, ahead, cur, prev, old):
                later_row, ahead_row, prev_row, old_row = (b and b.row(sp) for b in (later, ahead, prev, old))
                if prev:
                    if prev.c >= 2:
                        sp.wait_ge(stored[prev.parity], prev.turn(0))
                    if prev.c <= 1:
                        sp.wait_ge(weights_lo, 5)
                    sp.dma_start(resid[prev.parity], x[prev_row]).then_inc(resid_in[prev.parity], 16)
                if ahead:
                    sp.wait_ge(xn_lo, ahead.count(1, 1))
                    sp.dma_start(raw[:], ctx[ahead_row]).then_inc(raw_in, 16)
                    if ahead.c == 0:
                        load_piece(3)
                        load_piece(4)
                if cur:
                    sp.wait_ge(scores_done, cur.count(CHUNKS, 2))
                    place_q(1)
                if cur:
                    if cur.c >= 1:
                        sp.wait_ge(pv_done, cur.count(CHUNKS, 0))
                    else:
                        sp.wait_ge(v_diag_zero, 1)
                    sp.wait_ge(v_part3, cur.count(CHUNKS, 2))
                    place_v()
                if later:
                    if later.c >= 1:
                        sp.wait_ge(ctx_lo, later.count(1, 0))
                    sp.dma_start(raw[:], x[later_row]).then_inc(raw_in, 16)
                    if later.c == 0:
                        constants()
                        load_piece(1)
                        load_piece(2)
                if ahead:
                    if ahead.c >= 1:
                        sp.wait_ge(scores_done, ahead.count(CHUNKS, 0))
                    else:
                        sp.wait_ge(q_diag_zero, 1)
                    sp.wait_ge(q_part3, ahead.count(1, 1))
                    place_q(0)
                if cur:
                    sp.wait_ge(pv_done, cur.count(CHUNKS, 2))
                    sp.wait_ge(v_part3, cur.count(CHUNKS, 4))
                    place_v()
                if old:
                    sp.wait_ge(result_done, old.count(2, 2))
                    sp.dma_start(out[old_row], resid[old.parity]).then_inc(stored[old.parity], 16)

            steps(sp, step)
            sp.wait_ge(stored[0], 16 * (BATCHES // 2))
            sp.wait_ge(stored[1], 16 * (BATCHES // 2))

        @block.tensor
        def _(pe):
            pe.wait_ge(weights_lo, 1)
            pe.wait_ge(masks_ready, 2)
            pe.wait_ge(pads_zero, 4)

            def one_pass(n, dst, st, st_cols, mv, mv_cols, start, stop):
                s, m = ((0, 0), (0, 1), (1, 0))[n]
                return nc.tensor.matmul(dst, st[:, s, st_cols], mv[:, m, mv_cols],
                                        start=start and n == 0, stop=stop and n == 2)

            def product(*operands):
                for n in range(3):
                    last = one_pass(n, *operands)
                return last

            def project_pass(n, bank, which, source):
                half = slice(n // 3 * HALF, (n // 3 + 1) * HALF)
                return one_pass(n % 3, bank[:, half], w_split, slice(which * P, (which + 1) * P),
                                source, half, True, True)

            def tiles(m, s):
                return [(t, m % 2 * CT + t) for t in range(s * CT // GROUPS, (s + 1) * CT // GROUPS)]

            def open_scores(cur, m):
                if m >= 2 or cur.c >= 1:
                    pe.wait_ge(shifted, cur.count(CHUNKS, m - 1))
                nc.tensor.matmul(bank_b[m % 2][:], mask_rows[:], mask_cols[:],
                                 start=True, stop=False, skip_group_check=True)

            part_pairs = ((0, 2), (1, 1), (2, 0), (0, 1), (1, 0), (0, 0))

            def scores_group(m, s):
                for t, n in tiles(m, s):
                    at = (m * CT + t) * QT
                    for a, b in part_pairs:
                        last = nc.tensor.matmul(bank_b[m % 2][:, t * KT:(t + 1) * KT],
                                                q_diag[:, a, n:n + (P - 1) * HT + 1:HT],
                                                k_parts[:, b, at:at + KT], start=False,
                                                stop=t == CT - 1 and a == b == 0,
                                                skip_group_check=True)
                if s == GROUPS - 1:
                    last.then_inc(scores_done, 1)

            def weighted_group(m, s):
                for t, n in tiles(m, s):
                    at = (m * CT + t) * KT
                    for a, b in part_pairs:
                        last = nc.tensor.matmul(bank_b[2 + m % 2][:, t * PW:(t + 1) * PW],
                                                v_diag[:, a, n:n + (P - 1) * HT + 1:HT],
                                                prob_parts[:, b, at:at + KT],
                                                start=(a, b) == part_pairs[0], stop=a == b == 0)
                if s == GROUPS - 1:
                    last.then_inc(pv_done, 1)

            def transposes(bank, source, blocks):
                for f in blocks:
                    last = nc.tensor.transpose(bank[:, f * P:(f + 1) * P],
                                               source[:, f * P:(f + 1) * P], ident[:])
                return last

            def down(n, f):
                lo, hi = ((0, D1), (D1, DW))[n]
                last = product(bank_a[:, n * HALF:n * HALF + hi - lo], mid_split,
                               slice(f * P, (f + 1) * P), down_split,
                               slice(f * DW + lo, f * DW + hi), f == 0, f == FK - 1)
                if f == FK - 1:
                    last.then_inc(down_done, 1)

            def up(n, e):
                last = product(bank_a[:, n * HALF:(n + 1) * HALF], ht_split,
                               slice(e * P, (e + 1) * P), up_split,
                               slice(e * T + n * HALF, e * T + (n + 1) * HALF),
                               e == 0, e == EK - 1)
                if e == EK - 1:
                    last.then_inc(up_done, 1)

            def step(later, ahead, cur, prev, old):
                if cur:
                    if old:
                        pe.wait_ge(x1_done, old.count(2, 2))
                    else:
                        pe.wait_ge(k_out, cur.count(1, 1))
                    for n in range(6):
                        last = project_pass(n, bank_c, 2, src_split)
                    last.then_inc(v_done, 1)
                    pe.wait_ge(k_part3, cur.count(1, 1))
                    pe.wait_ge(q_placed, cur.count(32 * HEADS, 16 * HEADS))
                for m in range(2):
                    if cur:
                        open_scores(cur, m)
                    for s in range(GROUPS):
                        if cur:
                            scores_group(m, s)
                        if m == 1 and s == 1 and old:
                            pe.wait_ge(xn2_done, old.count(1, 1))
                            if old.c >= 1:
                                pe.wait_ge(result_done, old.count(2, 0))
                            transposes(bank_a, q_xn2, range(0, 4)).then_inc(xt_done, 1)
                            transposes(bank_a, q_xn2, range(4, FK)).then_inc(xt_done, 1)
                if prev:
                    pe.wait_ge(v_placed, prev.count(32 * PAIRS, 32 * PAIRS))
                for m in range(2, CHUNKS):
                    if prev:
                        pe.wait_ge(prob_part3, prev.count(CHUNKS, m + 1))
                        pe.wait_ge(attn_done, prev.count(CHUNKS, m - 1))
                    for s in range(GROUPS):
                        if prev:
                            weighted_group(m, s)
                        if m == 2 and ahead:
                            if s == 0:
                                pe.wait_ge(xn_hi, ahead.count(1, 1))
                                pe.wait_ge(xn_lo, ahead.count(1, 1))
                                if cur:
                                    pe.wait_ge(v_out, cur.count(1, 1))
                            for n in ((0, 1), (2,), (3, 4), (5,))[s]:
                                last = project_pass(n, bank_c, 0, src_split)
                            if s == GROUPS - 1:
                                last.then_inc(q_done, 1)
                        if old:
                            if m == 2 and s == 0:
                                pe.wait_ge(xt_hi, old.count(2, 2))
                                pe.wait_ge(xt_lo, old.count(2, 2))
                                if old.c == 0:
                                    pe.wait_ge(weights_lo, 5)
                            down(0, (m - 2) * GROUPS + s)
                if cur:
                    pe.wait_ge(q_placed, cur.count(32 * HEADS, 32 * HEADS))
                for m in range(2, CHUNKS):
                    if cur:
                        open_scores(cur, m)
                    for s in range(GROUPS):
                        if cur:
                            scores_group(m, s)
                        if m == 2 and old:
                            down(1, 2 * s)
                            down(1, 2 * s + 1)
                if cur:
                    pe.wait_ge(v_placed, cur.count(32 * PAIRS, 16 * PAIRS))
                for m in range(2):
                    if cur:
                        pe.wait_ge(prob_part3, cur.count(CHUNKS, m + 1))
                        if cur.c >= 1:
                            pe.wait_ge(attn_done, cur.count(CHUNKS, m - 1))
                    for s in range(GROUPS):
                        if cur:
                            weighted_group(m, s)
                        g = m * GROUPS + s
                        if g < 2 and ahead:
                            if g == 0:
                                pe.wait_ge(ctx_hi, ahead.count(1, 1))
                                pe.wait_ge(ctx_lo, ahead.count(1, 1))
                                pe.wait_ge(q_out, ahead.count(1, 1))
                            for n in range(3 * g, 3 * g + 3):
                                last = project_pass(n, bank_c, 1, src_split)
                            if g == 1:
                                last.then_inc(k_done, 1)
                        if g == 0 and old:
                            pe.wait_ge(h_done, old.count(2, 2))
                            transposes(bank_a, h_sb, range(EK)).then_inc(ht_done, 1)
                        if 3 <= g <= 5 and prev:
                            if g == 3:
                                pe.wait_ge(attn_hi, prev.count(1, 1))
                                pe.wait_ge(attn_lo, prev.count(1, 1))
                                if ahead:
                                    pe.wait_ge(k_out, ahead.count(1, 1))
                                elif cur:
                                    pe.wait_ge(v_out, cur.count(1, 1))
                            for n in (2 * g - 6, 2 * g - 5):
                                last = project_pass(n, bank_c, 3, mid_split)
                                if n % 3 == 2:
                                    last.then_inc(o_done, 1)
                        if old:
                            if g == 2:
                                pe.wait_ge(ht_hi, old.count(1, 1))
                                pe.wait_ge(ht_lo, old.count(1, 1))
                            for n in ((), (), (0,), (1,), (2,), (3,), (4, 5), (6, 7))[g]:
                                up(*divmod(n, EK))

            steps(pe, step)

        @block.scalar
        def _(act):
            def split_hi(n):
                _, exact, parts = pieces[n]
                act.wait_ge(weights_in[n], 16)
                nc.scalar.activation(parts[:, 0, :], exact, ACT.Copy).then_inc(weights_hi, 1)

            split_hi(0)
            act.wait_ge(small_in, 16 * 4)
            nc.scalar.activation(mask_rows[:], prob[:, 0:P], ACT.Copy).then_inc(masks_ready, 1)
            nc.scalar.activation(mask_cols[:], prob[:, P:P + CW], ACT.Copy).then_inc(masks_ready, 1)
            nc.scalar.activation(bq_scaled[:], bias[:, 0:1], ACT.Copy, scale=SCALE).then_inc(bq_ready, 1)

            def even_heads(b, m):
                act.wait_ge(pv_done, b.count(CHUNKS, m + 1))
                if m == 0 and b.c >= 1:
                    act.wait_ge(attn_lo, b.count(1, 0))
                src = bank_b[2 + m % 2][:].rearrange("p (n h i) -> p n h i", h=2, i=QT)
                dst = attn[:, m * CT * QT:(m + 1) * CT * QT]
                nc.scalar.activation(dst.rearrange("p (n i) -> p n i", i=QT), src[:, :, 0, :],
                                     ACT.Copy, scale=consts[:, 0:1]).then_inc(even_out, 1)

            def exponentials(cur, m):
                act.wait_ge(shifted, cur.count(CHUNKS, m + 1))
                half = slice(m % 2 * CW, (m % 2 + 1) * CW)
                nc.scalar.activation(prob[:, half], prob[:, half], ACT.Exp).then_inc(exp_done, 1)

            def weights_part1(b, m):
                at = m % 2 * CW
                act.wait_ge(prob_t_done, b.count(CHUNKS, m + 1))
                if b.c >= 1:
                    act.wait_ge(pv_done, b.count(CHUNKS, m - 3))
                elif m == 0:
                    act.wait_ge(weights_lo, 4)
                nc.scalar.activation(prob_parts[:, 0, m * CW:(m + 1) * CW], prob_t[:, at:at + CW],
                                     ACT.Copy).then_inc(prob_part1, 1)

            def weights_part2(b, m):
                at = m % 2 * CW
                act.wait_ge(prob_rest, b.count(CHUNKS, m + 1))
                nc.scalar.activation(prob_parts[:, 1, m * CW:(m + 1) * CW], prob_t[:, at:at + CW],
                                     ACT.Copy).then_inc(prob_part2, 1)

            def v_first(cur, half):
                act.wait_ge(v_t_done, cur.count(2, half + 1))
                if half or cur.c >= 1:
                    act.wait_ge(v_placed, cur.count(32 * PAIRS, 16 * PAIRS * half))
                nc.scalar.activation(v_parts[:, 0, :], v_t[:], ACT.Copy).then_inc(v_part1, 1)

            def v_second(cur, half):
                act.wait_ge(v_rest, cur.count(2, half + 1))
                nc.scalar.activation(v_parts[:, 1, :], v_t[:], ACT.Copy).then_inc(v_part2, 1)

            def step(later, ahead, cur, prev, old):
                if cur:
                    act.wait_ge(v_done, cur.count(1, 1))
                    act.wait_ge(k_part3, cur.count(1, 1))
                    nc.scalar.activation(kv_sb[:, PAD_LEFT:PAD_LEFT + T], bank_c[:], ACT.Identity,
                                         bias=bias[:, 2:3]).then_inc(v_out, 1)
                if old:
                    for n in range(2):
                        act.wait_ge(xt_done, old.count(2, n + 1))
                        if n == 0:
                            act.wait_ge(o_done, old.count(2, 2))
                        half = slice(n * HALF, (n + 1) * HALF)
                        nc.scalar.activation(mid_split[:, 0, half], bank_a[:, half],
                                             ACT.Copy).then_inc(xt_hi, 1)
                if prev:
                    weights_part2(prev, 3)
                if cur:
                    if cur.c == 0:
                        split_hi(3)
                        split_hi(4)
                    exponentials(cur, 0)
                    exponentials(cur, 1)
                    weights_part1(cur, 0)
                    v_first(cur, 0)
                if ahead:
                    act.wait_ge(q_done, ahead.count(1, 1))
                    if old:
                        act.wait_ge(xt_done, old.count(2, 2))
                    elif ahead.c >= 1:
                        act.wait_ge(q_part3, ahead.count(1, 0))
                    if ahead.c == 0:
                        act.wait_ge(bq_ready, 1)
                    nc.scalar.activation(q_xn2[:].rearrange("p (h i n) -> p h n i", h=2, n=HT),
                                         bank_c[:].rearrange("p (h n i) -> p h n i", h=2, i=QT),
                                         ACT.Identity, bias=bq_scaled[:], scale=SCALE).then_inc(q_out, 1)
                if cur:
                    weights_part2(cur, 0)
                    v_second(cur, 0)
                if ahead:
                    act.wait_ge(q_out, ahead.count(1, 1))
                    if ahead.c >= 1:
                        act.wait_ge(q_placed, ahead.count(32 * HEADS, 0))
                    nc.scalar.activation(q_parts[:, 0, :], q_xn2[:], ACT.Copy).then_inc(q_part1, 1)
                if prev:
                    even_heads(prev, 2)
                if cur:
                    weights_part1(cur, 1)
                if ahead:
                    act.wait_ge(q_rest, ahead.count(1, 1))
                    nc.scalar.activation(q_parts[:, 1, :], q_xn2[:], ACT.Copy).then_inc(q_part2, 1)
                    if ahead.c == 0:
                        split_hi(1)
                        split_hi(2)
                if prev:
                    even_heads(prev, 3)
                if old:
                    act.wait_ge(gate_step, old.count(13, 7))
                    nc.scalar.activation(gate[:, 1:2], gate[:, 0:1], ACT.Exp).then_inc(gap_exp, 1)
                if cur:
                    weights_part2(cur, 1)
                if old:
                    act.wait_ge(ht_done, old.count(1, 1))
                    if old.c >= 1:
                        act.wait_ge(up_done, old.count(2, 0))
                    nc.scalar.activation(ht_split[:, 0, :], bank_a[:, 0:ER], ACT.Copy).then_inc(ht_hi, 1)
                if cur:
                    exponentials(cur, 2)
                if ahead:
                    act.wait_ge(k_done, ahead.count(1, 1))
                    if cur:
                        act.wait_ge(v_t_done, cur.count(2, 2))
                    nc.scalar.activation(kv_sb[:, PAD_LEFT:PAD_LEFT + T], bank_c[:], ACT.Identity,
                                         bias=bias[:, 1:2]).then_inc(k_out, 1)
                    act.wait_ge(k_out, ahead.count(1, 1))
                    if ahead.c >= 1:
                        act.wait_ge(scores_done, ahead.count(CHUNKS, 0))
                    nc.scalar.activation(k_parts[:, 0, PAD_LEFT:PAD_LEFT + T], kv_sb[:, PAD_LEFT:PAD_LEFT + T],
                                         ACT.Copy).then_inc(k_part1, 1)
                if cur:
                    exponentials(cur, 3)
                    v_first(cur, 1)
                    weights_part1(cur, 2)
                if ahead:
                    act.wait_ge(k_rest, ahead.count(1, 1))
                    nc.scalar.activation(k_parts[:, 1, PAD_LEFT:PAD_LEFT + T], kv_sb[:, PAD_LEFT:PAD_LEFT + T],
                                         ACT.Copy).then_inc(k_part2, 1)
                if cur:
                    weights_part2(cur, 2)
                    even_heads(cur, 0)
                    v_second(cur, 1)
                if prev:
                    act.wait_ge(ln2_step, prev.count(6, 6))
                    if ahead:
                        act.wait_ge(q_part3, ahead.count(1, 1))
                    elif old:
                        act.wait_ge(xt_done, old.count(2, 2))
                    nc.scalar.activation(q_xn2[:], resid[prev.parity], ACT.Identity, bias=shift[:, 1:2],
                                         scale=rstd[:, 1:2]).then_inc(xn2_done, 1)
                if later:
                    act.wait_ge(ln1_step, later.count(6, 6))
                    nc.scalar.activation(raw[:], raw[:], ACT.Identity, bias=shift[:, 0:1],
                                         scale=rstd[:, 0:1]).then_inc(xn_done, 1)
                if cur:
                    weights_part1(cur, 3)
                    even_heads(cur, 1)

            steps(act, step)

        @block.vector
        def _(dve):
            def split_lo(n):
                _, exact, parts = pieces[n]
                dve.wait_ge(weights_hi, n + 1)
                nc.vector.tensor_tensor(parts[:, 1, :], exact, parts[:, 0, :].bitcast(F32),
                                        ALU.subtract).then_inc(weights_lo, 1)

            split_lo(0)
            dve.wait_ge(small_in, 16 * 4)

            def fence(semaphore, which):
                nc.vector.memset(fences[:, which:which + 1], 0.0).then_inc(semaphore, 1)

            def layernorm_stats(which, source, semaphore, batch):
                for n in range(2):
                    nc.vector.bn_stats(stats[:, which, n, :],
                                       source[:, n * HALF:(n + 1) * HALF]).then_inc(semaphore, 1)
                dve.wait_ge(semaphore, batch.count(6, 2))
                fence(semaphore, which)
                nc.vector.bn_aggr(moments[:, which, :],
                                  stats[:, which, :, :].rearrange("p a b -> p (a b)")).then_inc(semaphore, 1)
                dve.wait_ge(semaphore, batch.count(6, 4))
                nc.vector.tensor_scalar(var_eps[:, which:which + 1], moments[:, which, 1:2], EPS, None,
                                        ALU.add).then_inc(semaphore, 1)

            def layernorm_shift(which, semaphore, batch):
                nc.vector.scalar_tensor_tensor(shift[:, which:which + 1], moments[:, which, 0:1], -1.0,
                                               rstd[:, which:which + 1], ALU.mult,
                                               ALU.mult).then_inc(semaphore, 1)

            def join_heads(prev, m):
                dve.wait_ge(even_out, prev.count(CHUNKS, m + 1))
                src = bank_b[2 + m % 2][:].rearrange("p (n h i) -> p n h i", h=2, i=QT)
                dst = attn[:, m * CT * QT:(m + 1) * CT * QT].rearrange("p (n i) -> p n i", i=QT)
                nc.vector.scalar_tensor_tensor(dst, src[:, :, 1, :], consts[:, 1:2], dst,
                                               ALU.mult, ALU.add).then_inc(attn_done, 1)

            def choose_experts(old):
                dve.wait_ge(down_done, old.count(2, 1))
                nc.vector.tensor_copy(logits[:], bank_a[:, ER2:D1]).then_inc(gate_step, 1)
                dve.wait_ge(gate_step, old.count(13, 1))
                fence(gate_step, 2)
                nc.vector.max(top[:], logits[:]).then_inc(gate_step, 1)
                dve.wait_ge(gate_step, old.count(13, 3))
                fence(gate_step, 2)
                nc.vector.max_index(top_at[:], top[:], logits[:]).then_inc(gate_step, 1)
                dve.wait_ge(gate_step, old.count(13, 5))
                nc.vector.tensor_copy(top_atf[:], top_at[:, 0:2]).then_inc(gate_step, 1)
                nc.vector.tensor_tensor(gate[:, 0:1], top[:, 1:2], top[:, 0:1],
                                        ALU.subtract).then_inc(gate_step, 1)
                dve.wait_ge(gap_exp, old.count(1, 1))
                nc.vector.tensor_scalar(gate[:, 2:3], gate[:, 1:2], 1.0, None, ALU.add).then_inc(gate_step, 1)
                dve.wait_ge(gate_step, old.count(13, 8))
                nc.vector.reciprocal(gate[:, 3:4], gate[:, 2:3]).then_inc(gate_step, 1)
                dve.wait_ge(gate_step, old.count(13, 9))
                nc.vector.tensor_tensor(gate[:, 4:5], gate[:, 1:2], gate[:, 3:4], ALU.mult).then_inc(gate_step, 1)
                dve.wait_ge(gate_step, old.count(13, 10))
                for n in range(2):
                    nc.vector.tensor_scalar(pick[:, n, :], consts[:, 4:4 + EXPERTS],
                                            top_atf[:, n:n + 1], gate[:, 3 + n:4 + n],
                                            ALU.is_equal, ALU.mult).then_inc(gate_step, 1)
                dve.wait_ge(gate_step, old.count(13, 12))
                nc.vector.tensor_tensor(pick[:, 2, :], pick[:, 0, :], pick[:, 1, :],
                                        ALU.add).then_inc(gate_step, 1)
                dve.wait_ge(gate_step, old.count(13, 13))

            def weigh_experts(old, n):
                experts = slice(n * EXPERTS // 2, (n + 1) * EXPERTS // 2)
                dve.wait_ge(down_done, old.count(2, n + 1))
                if n == 0 and old.c >= 1:
                    dve.wait_ge(ht_done, old.count(1, 0))
                nc.vector.tensor_tensor(
                    h_sb[:, n * ER2:(n + 1) * ER2].rearrange("p (e r) -> p e r", r=RANK),
                    bank_a[:, n * HALF:n * HALF + ER2].rearrange("p (e r) -> p e r", r=RANK),
                    pick[:, 2, experts].unsqueeze(2).broadcast_to([P, EXPERTS // 2, RANK]),
                    ALU.mult).then_inc(h_done, 1)

            def scores_shift(cur, m):
                cols = slice(m * CT, (m + 1) * CT)
                scores = bank_b[m % 2][:].rearrange("p (n j) -> p n j", j=KT)
                dve.wait_ge(scores_done, cur.count(CHUNKS, m + 1))
                nc.vector.tensor_reduce(row_max[:, cols], scores, AX_X, ALU.max).then_inc(max_done, 1)
                dve.wait_ge(max_done, cur.count(CHUNKS, m + 1))
                if m >= 2 or cur.c >= 1:
                    dve.wait_ge(prob_t_done, cur.count(CHUNKS, m - 1))
                nc.vector.tensor_tensor(prob[:, m % 2 * CW:(m % 2 + 1) * CW].rearrange("p (n j) -> p n j", j=KT), scores,
                                        row_max[:, cols].unsqueeze(2).broadcast_to([P, CT, KT]),
                                        ALU.subtract).then_inc(shifted, 1)

            def weights_sum(cur, m):
                cols = slice(m * CT, (m + 1) * CT)
                dve.wait_ge(exp_done, cur.count(CHUNKS, m + 1))
                nc.vector.tensor_reduce(row_sum[:, cols],
                                        prob[:, m % 2 * CW:(m % 2 + 1) * CW].rearrange("p (n j) -> p n j", j=KT),
                                        AX_X, ALU.add).then_inc(sum_done, 1)
                dve.wait_ge(sum_done, cur.count(CHUNKS, m + 1))
                if m == 0 and cur.c >= 1:
                    dve.wait_ge(prob_done, cur.count(CHUNKS, 0))
                nc.vector.reciprocal(row_inv[:, cols], row_sum[:, cols]).then_inc(inv_done, 1)

            def weights_transpose(cur, m):
                at = m % 2 * CW
                dve.wait_ge(prob_done, cur.count(CHUNKS, m + 1))
                if m >= 2 or cur.c >= 1:
                    dve.wait_ge(prob_part3, cur.count(CHUNKS, m - 1))
                nc.vector.transpose(prob_t[:, at:at + CW], prob[:, at:at + CW]).then_inc(prob_t_done, 1)

            def weights_rest(b, m):
                tile = prob_t[:, m % 2 * CW:(m % 2 + 1) * CW]
                dve.wait_ge(prob_part1, b.count(CHUNKS, m + 1))
                nc.vector.tensor_tensor(tile, tile, prob_parts[:, 0, m * CW:(m + 1) * CW],
                                        ALU.subtract).then_inc(prob_rest, 1)

            def weights_part3(b, m):
                cols = slice(m * CW, (m + 1) * CW)
                dve.wait_ge(prob_part2, b.count(CHUNKS, m + 1))
                nc.vector.tensor_tensor(prob_parts[:, 2, cols], prob_t[:, m % 2 * CW:(m % 2 + 1) * CW],
                                        prob_parts[:, 1, cols], ALU.subtract).then_inc(prob_part3, 1)

            def v_transpose(cur, half):
                dve.wait_ge(v_out, cur.count(1, 1))
                if half or cur.c >= 1:
                    dve.wait_ge(v_part3, cur.count(CHUNKS, 2 * half))
                windows = bass.AP(tensor=kv_sb[:].tensor, offset=half * HT * QT,
                                  ap=[[KPAD, P], [QT, HT], [1, KT]])
                nc.vector.transpose(v_t[:].rearrange("p (c n) -> p n c", n=HT),
                                    windows).then_inc(v_t_done, 1)

            def v_leave(cur, half):
                dve.wait_ge(v_part1, cur.count(2, half + 1))
                nc.vector.tensor_tensor(v_t[:], v_t[:], v_parts[:, 0, :], ALU.subtract).then_inc(v_rest, 1)

            def v_third(cur, half):
                dve.wait_ge(v_part2, cur.count(2, half + 1))
                nc.vector.tensor_tensor(v_parts[:, 2, :], v_t[:], v_parts[:, 1, :],
                                        ALU.subtract).then_inc(v_part3, 2)

            def add_mixture(old, n):
                y = resid[old.parity][:, n * HALF:(n + 1) * HALF]
                dve.wait_ge(up_done, old.count(2, n + 1))
                nc.vector.tensor_tensor(y, bank_a[:, n * HALF:(n + 1) * HALF], y,
                                        ALU.add).then_inc(result_done, 1)

            def step(later, ahead, cur, prev, old):
                if ahead:
                    dve.wait_ge(xn_done, ahead.count(1, 1))
                    if cur:
                        dve.wait_ge(v_done, cur.count(1, 1))
                    nc.vector.tensor_copy(src_split[:, 0, :], raw[:]).then_inc(xn_hi, 1)
                if prev:
                    join_heads(prev, 1)
                    weights_rest(prev, 3)
                if old:
                    for n in range(2):
                        half = slice(n * HALF, (n + 1) * HALF)
                        dve.wait_ge(xt_hi, old.count(2, n + 1))
                        nc.vector.tensor_tensor(mid_split[:, 1, half], bank_a[:, half],
                                                mid_split[:, 0, half].bitcast(F32),
                                                ALU.subtract).then_inc(xt_lo, 1)
                if prev:
                    weights_part3(prev, 3)
                if cur:
                    scores_shift(cur, 0)
                    if cur.c == 0:
                        split_lo(3)
                    weights_sum(cur, 0)
                    v_transpose(cur, 0)
                    scores_shift(cur, 1)
                    weights_transpose(cur, 0)
                    weights_sum(cur, 1)
                    weights_rest(cur, 0)
                    v_leave(cur, 0)
                if ahead:
                    dve.wait_ge(raw_in, ahead.count(32, 32))
                    dve.wait_ge(q_done, ahead.count(1, 1))
                    nc.vector.tensor_copy(src_split[:, 0, :], raw[:]).then_inc(ctx_hi, 1)
                    if ahead.c == 0:
                        split_lo(1)
                        split_lo(2)
                if cur:
                    weights_transpose(cur, 1)
                    weights_part3(cur, 0)
                    v_third(cur, 0)
                if prev:
                    join_heads(prev, 2)
                if cur:
                    weights_rest(cur, 1)
                    v_transpose(cur, 1)
                if old:
                    choose_experts(old)
                    weigh_experts(old, 0)
                if prev:
                    join_heads(prev, 3)
                if cur:
                    weights_part3(cur, 1)
                if old:
                    weigh_experts(old, 1)
                if prev:
                    dve.wait_ge(attn_done, prev.count(CHUNKS, CHUNKS))
                    if old:
                        dve.wait_ge(down_done, old.count(2, 2))
                    nc.vector.tensor_copy(mid_split[:, 0, :], attn[:]).then_inc(attn_hi, 1)
                if cur:
                    scores_shift(cur, 2)
                if old:
                    dve.wait_ge(ht_hi, old.count(1, 1))
                    nc.vector.tensor_tensor(ht_split[:, 1, :], bank_a[:, 0:ER],
                                            ht_split[:, 0, :].bitcast(F32),
                                            ALU.subtract).then_inc(ht_lo, 1)
                if cur:
                    weights_sum(cur, 2)
                    scores_shift(cur, 3)
                    weights_transpose(cur, 2)
                    weights_sum(cur, 3)
                    weights_rest(cur, 2)
                if prev:
                    x1 = resid[prev.parity]
                    dve.wait_ge(resid_in[prev.parity], prev.turn(1))
                    for n in range(2):
                        half = slice(n * HALF, (n + 1) * HALF)
                        dve.wait_ge(o_done, prev.count(2, n + 1))
                        nc.vector.scalar_tensor_tensor(x1[:, half], bank_c[:, half], bias[:, 3:4],
                                                       x1[:, half], ALU.add,
                                                       ALU.add).then_inc(x1_done, 1)
                    dve.wait_ge(x1_done, prev.count(2, 2))
                    layernorm_stats(1, x1, ln2_step, prev)
                if cur:
                    weights_part3(cur, 2)
                if later:
                    dve.wait_ge(raw_in, later.count(32, 16))
                    layernorm_stats(0, raw, ln1_step, later)
                if prev:
                    dve.wait_ge(rstd2, prev.count(1, 1))
                    layernorm_shift(1, ln2_step, prev)
                if cur:
                    join_heads(cur, 0)
                if later:
                    dve.wait_ge(rstd1, later.count(1, 1))
                    layernorm_shift(0, ln1_step, later)
                if cur:
                    weights_transpose(cur, 3)
                if old:
                    add_mixture(old, 0)
                    add_mixture(old, 1)
                if cur and cur.c == 0:
                    split_lo(4)

            steps(dve, step)

        @block.gpsimd
        def _(pool):
            for padded in (k_parts[:], kv_sb[:].unsqueeze(1)):
                nc.gpsimd.memset(padded[:, :, 0:PAD_LEFT], 0.0).then_inc(pads_zero, 1)
                nc.gpsimd.memset(padded[:, :, PAD_LEFT + T:KPAD], 0.0).then_inc(pads_zero, 1)
            nc.gpsimd.memset(q_diag[:].rearrange("p a n -> p (a n)").bitcast(F32),
                             0.0).then_inc(q_diag_zero, 1)
            pool.wait_ge(small_in, 16 * 4)

            def weights_norm(cur, m):
                cols = slice(m * CT, (m + 1) * CT)
                pool.wait_ge(inv_done, cur.count(CHUNKS, m + 1))
                p3 = prob[:, m % 2 * CW:(m % 2 + 1) * CW].rearrange("p (n j) -> p n j", j=KT)
                nc.gpsimd.tensor_tensor(p3, p3, row_inv[:, cols].unsqueeze(2).broadcast_to([P, CT, KT]),
                                        ALU.mult).then_inc(prob_done, 1)

            def v_leave(cur, half):
                pool.wait_ge(v_part1, cur.count(2, half + 1))
                nc.gpsimd.tensor_tensor(v_t[:], v_t[:], v_parts[:, 0, :], ALU.subtract).then_inc(v_rest, 1)

            def v_third(cur, half):
                pool.wait_ge(v_part2, cur.count(2, half + 1))
                nc.gpsimd.tensor_tensor(v_parts[:, 2, :], v_t[:], v_parts[:, 1, :],
                                        ALU.subtract).then_inc(v_part3, 2)

            def step(later, ahead, cur, prev, old):
                if ahead:
                    pool.wait_ge(xn_hi, ahead.count(1, 1))
                    nc.gpsimd.tensor_tensor(src_split[:, 1, :], raw[:], src_split[:, 0, :].bitcast(F32),
                                            ALU.subtract).then_inc(xn_lo, 1)
                if cur:
                    if cur.c == 0:
                        pool.wait_ge(weights_lo, 3)
                        nc.gpsimd.memset(v_diag_f32, 0.0).then_inc(v_diag_zero, 1)
                    weights_norm(cur, 0)
                    weights_norm(cur, 1)
                if ahead:
                    pool.wait_ge(q_part1, ahead.count(1, 1))
                    nc.gpsimd.tensor_tensor(q_xn2[:], q_xn2[:], q_parts[:, 0, :],
                                            ALU.subtract).then_inc(q_rest, 1)
                if ahead:
                    pool.wait_ge(ctx_hi, ahead.count(1, 1))
                    nc.gpsimd.tensor_tensor(src_split[:, 1, :], raw[:], src_split[:, 0, :].bitcast(F32),
                                            ALU.subtract).then_inc(ctx_lo, 1)
                if ahead:
                    pool.wait_ge(q_part2, ahead.count(1, 1))
                    nc.gpsimd.tensor_tensor(q_parts[:, 2, :], q_xn2[:], q_parts[:, 1, :],
                                            ALU.subtract).then_inc(q_part3, 1)
                if prev:
                    pool.wait_ge(attn_hi, prev.count(1, 1))
                    nc.gpsimd.tensor_tensor(mid_split[:, 1, :], attn[:], mid_split[:, 0, :].bitcast(F32),
                                            ALU.subtract).then_inc(attn_lo, 1)
                if cur:
                    weights_norm(cur, 2)
                if ahead:
                    pool.wait_ge(k_part1, ahead.count(1, 1))
                    nc.gpsimd.tensor_tensor(kv_sb[:, PAD_LEFT:PAD_LEFT + T], kv_sb[:, PAD_LEFT:PAD_LEFT + T],
                                            k_parts[:, 0, PAD_LEFT:PAD_LEFT + T],
                                            ALU.subtract).then_inc(k_rest, 1)
                if cur:
                    weights_norm(cur, 3)
                if ahead:
                    k_part = k_parts[:, :, PAD_LEFT:PAD_LEFT + T]
                    pool.wait_ge(k_part2, ahead.count(1, 1))
                    nc.gpsimd.tensor_tensor(k_part[:, 2, :], kv_sb[:, PAD_LEFT:PAD_LEFT + T], k_part[:, 1, :],
                                            ALU.subtract).then_inc(k_part3, 1)
                if cur:
                    v_leave(cur, 1)
                if prev:
                    pool.wait_ge(ln2_step, prev.count(6, 5))
                    nc.gpsimd.tensor_tensor(rstd[:, 1:2], var_eps[:, 1:2], consts[:, 2:3],
                                            ALU.pow).then_inc(rstd2, 1)
                if cur:
                    v_third(cur, 1)
                if later:
                    pool.wait_ge(ln1_step, later.count(6, 5))
                    nc.gpsimd.tensor_tensor(rstd[:, 0:1], var_eps[:, 0:1], consts[:, 2:3],
                                            ALU.pow).then_inc(rstd1, 1)

            steps(pool, step)


def shape_constants():
    rows = np.arange(P)
    mask_rows = (rows[:, None] == rows[None, :] % QT).astype(np.float32)
    key = np.arange(CW) % KT
    inside = (key[None, :] >= rows[:, None]) & (key[None, :] < rows[:, None] + WINDOW)
    mask_cols = np.where(inside | (rows[:, None] >= QT), 0.0, MASKED).astype(np.float32)
    consts = np.zeros((P, 4 + EXPERTS), np.float32)
    consts[:, 0] = rows // HD % 2 == 0
    consts[:, 1] = rows // HD % 2 == 1
    consts[:, 2] = -0.5
    consts[:, 3] = EPS
    consts[:, 4:] = np.arange(EXPERTS)
    return np.eye(P, dtype=np.float32), np.concatenate([mask_rows, mask_cols], axis=1), consts


def kernel(**inputs):
    import numpy as np
    import concourse.bacc as bacc
    from concourse import mybir
    from concourse.bass_utils import run_bass_kernel_spmd

    a = {k: np.asarray(v) for k, v in inputs.items()}
    x, ctx = a["x"], a["ctx_4096"]
    wqkvo = np.concatenate([a[f"L0_xattn_W{n}"].T for n in "qkvo"], axis=1)
    biases = np.stack([a[f"L0_xattn_b{n}"] for n in "qkvo"], axis=1)
    down = a["L0_ffn_lora_A"].reshape(ER, T)
    down = np.concatenate([down[:ER2], a["L0_ffn_gate_w"], down[ER2:]], axis=0)
    down = down.T.reshape(FK, P, DW).transpose(1, 0, 2).reshape(P, FK * DW)
    up = a["L0_ffn_lora_B"].transpose(0, 2, 1).reshape(EK, P, T).transpose(1, 0, 2).reshape(P, EK * T)
    ident, masks, consts = shape_constants()

    arrays = {
        "x": x, "ctx": ctx, "wqkvo": wqkvo, "biases": biases, "down_w": down, "up_w": up,
        "ident_in": ident, "masks_in": masks, "consts_in": consts,
    }
    arrays = {k: np.ascontiguousarray(v) for k, v in arrays.items()}
    nc = bacc.Bacc("TRN2", target_bir_lowering=False, num_devices=1)
    args = [nc.dram_tensor(k, v.shape, mybir.dt.from_np(v.dtype), kind="ExternalInput").ap()
            for k, v in arrays.items()]
    out = nc.dram_tensor("out", x.shape, mybir.dt.float32, kind="ExternalOutput").ap()
    build(nc, *args, out)
    r = run_bass_kernel_spmd(nc, [arrays], core_ids=[0])
    return r.results[0]["out"]
```
